# Optimizing a Trainium2 kernel written in Bass

```python
import numpy as np
import jax
import jax.numpy as jnp

def _softmax(x, axis=-1):
    return jax.nn.softmax(x, axis=axis)

def _gelu(x):
    return jax.nn.gelu(x, approximate=True)

def _silu(x):
    return jax.nn.silu(x)

def _sigmoid(x):
    return jax.nn.sigmoid(x)

def _layernorm(x, axis=-1, eps=1e-05):
    m = jnp.mean(x, axis=axis, keepdims=True)
    v = jnp.var(x, axis=axis, keepdims=True)
    return (x - m) / jnp.sqrt(v + eps)

def _scatter_add(tgt, idx, src, axis=0):
    return tgt.at[idx].add(src)

def _segment_sum(src, seg, n):
    return jax.ops.segment_sum(src, seg, n)
kernel_name = 'mk_flamingo_gated_d1_seqx_r4_3d40e8'

def setup_inputs(seed: int=0):
    np.random.seed(seed)
    _w = jnp.asarray

    def _rec_inputs():
        import jax
        import jax.numpy as jnp
        _rk = jax.random.key(seed)
        x = 7.22e-05 + 1 * jax.random.normal(jax.random.fold_in(_rk, 1), (32, 128, 256), jnp.float32)
        _lenS = 128 - jax.random.randint(jax.random.fold_in(_rk, 7), (32,), 0, max(1, 128 // 4) + 1, jnp.int32)
        _lenS2 = 128 - jax.random.randint(jax.random.fold_in(_rk, 8), (32,), 0, max(1, 128 // 4) + 1, jnp.int32)
        _ctx_1024P = jax.random.normal(jax.random.fold_in(_rk, 11), (32, 16, 256), jnp.float32)
        _ctx_1024c = jax.random.dirichlet(jax.random.fold_in(_rk, 511), 0.3 * jnp.ones((16,), jnp.float32), (32, 128))
        _ctx_1024t = jnp.einsum('bsk,bkd->bsd', _ctx_1024c, _ctx_1024P)
        _ctx_1024t = _ctx_1024t * jax.lax.rsqrt(jnp.mean(jnp.square(_ctx_1024t)) + 1e-12) * 0.953939
        ctx_1024 = 4.13588e-05 + 0.999923 * (_ctx_1024t + 0.3 * jax.random.normal(jax.random.fold_in(_rk, 611), (32, 128, 256), jnp.float32))
        _validS = jnp.arange(128)[None, :] < _lenS[:, None]
        _validS2 = jnp.arange(128)[None, :] < _lenS2[:, None]
        _causal = jnp.tril(jnp.ones((128, 128), dtype=bool))
        mask_Bx1xSxS2_bk1 = jnp.broadcast_to(_validS2[:, None, None, :], (32, 1, 128, 128))
        _g = jax.random.normal(jax.random.fold_in(_rk, 9001), (2, 1), jnp.float32)
        _g = jnp.sign(_g) * jnp.maximum(jnp.abs(_g), 1.0) + (_g == 0) * 1.0
        g_xattn = _g[0]
        g_ffn = _g[1]
        return (x, ctx_1024, mask_Bx1xSxS2_bk1, g_xattn, g_ffn)
    x, ctx_1024, mask_Bx1xSxS2_bk1, g_xattn, g_ffn = _rec_inputs()

    def _L0_xattn_setup():
        import jax, jax.numpy as jnp
        import numpy as np
        EMBED = 256
        HEADS = 16
        HEAD_DIM = EMBED // HEADS
        B, S = (4, 512)

        def _split_heads(x):
            b, s, _ = x.shape
            return x.reshape(b, s, HEADS, HEAD_DIM).transpose(0, 2, 1, 3)
        key = jax.random.key(seed)
        ks = jax.random.split(key, 13)
        scale = 1.0 / np.sqrt(EMBED)
        inp = {'query': jax.random.normal(ks[0], (B, S, EMBED), dtype=jnp.float32), 'key': jax.random.normal(ks[1], (B, S, EMBED), dtype=jnp.float32), 'value': jax.random.normal(ks[2], (B, S, EMBED), dtype=jnp.float32), 'mask': jax.random.randint(ks[3], (B, 1, S, S), 0, 2) > 0, 'Wq': jax.random.normal(ks[4], (EMBED, EMBED), dtype=jnp.float32) * scale, 'bq': jnp.zeros((EMBED,), dtype=jnp.float32), 'Wk': jax.random.normal(ks[5], (EMBED, EMBED), dtype=jnp.float32) * scale, 'bk': jnp.zeros((EMBED,), dtype=jnp.float32), 'Wv': jax.random.normal(ks[6], (EMBED, EMBED), dtype=jnp.float32) * scale, 'bv': jnp.zeros((EMBED,), dtype=jnp.float32), 'Wo': jax.random.normal(ks[7], (EMBED, EMBED), dtype=jnp.float32) * scale, 'bo': jnp.zeros((EMBED,), dtype=jnp.float32)}
        return inp
    _L0_xattn_all = _L0_xattn_setup()
    _L0_xattn_in = {k: v for k, v in _L0_xattn_all.items() if k in ('Wq', 'bq', 'Wk', 'bk', 'Wv', 'bv', 'Wo', 'bo')}
    del _L0_xattn_all

    def _L0_ffn_setup():
        import jax, jax.numpy as jnp
        import numpy as np
        NUM_HEADS = 16
        TOP_K = 2
        ROPE_BASE = 10000.0
        LN_EPS = 1e-05

        def _rope_sin_cos(S, D, dtype):
            inv_freq = 1.0 / ROPE_BASE ** (jnp.arange(0, D, 2, dtype=jnp.float32) / D)
            freqs = jnp.arange(S, dtype=jnp.float32)[:, None] * inv_freq[None, :]
            sin = jnp.sin(freqs).astype(dtype)[None, :, None, :]
            cos = jnp.cos(freqs).astype(dtype)[None, :, None, :]
            return (sin, cos)

        def _apply_rope(x, sin, cos):
            x1, x2 = (x[..., 0::2], x[..., 1::2])
            r1 = x1 * cos - x2 * sin
            r2 = x1 * sin + x2 * cos
            return jnp.stack([r1, r2], axis=-1).reshape(x.shape)

        def _layer_norm(x, w, b):
            mu = jnp.mean(x, axis=-1, keepdims=True)
            var = jnp.mean(jnp.square(x - mu), axis=-1, keepdims=True)
            return (x - mu) * jax.lax.rsqrt(var + LN_EPS) * w + b
        key = jax.random.key(seed)
        ks = jax.random.split(key, 8)
        B, S, E, NE = (2, 512, 256, 8)
        s = 0.02
        return {'x': jax.random.normal(ks[0], (B, S, E), dtype=jnp.float32), 'in_proj_w': jax.random.normal(ks[1], (3 * E, E), dtype=jnp.float32) * s, 'in_proj_b': jnp.zeros((3 * E,), dtype=jnp.float32), 'out_proj_w': jax.random.normal(ks[2], (E, E), dtype=jnp.float32) * s, 'out_proj_b': jnp.zeros((E,), dtype=jnp.float32), 'gate_w': jax.random.normal(ks[3], (NE, E), dtype=jnp.float32) * s, 'gate_b': jnp.zeros((NE,), dtype=jnp.float32), 'expert_w': jax.random.normal(ks[4], (NE, E, E), dtype=jnp.float32) * s, 'expert_b': jnp.zeros((NE, E), dtype=jnp.float32), 'ln1_w': jnp.ones((E,), dtype=jnp.float32), 'ln1_b': jnp.zeros((E,), dtype=jnp.float32), 'ln2_w': jnp.ones((E,), dtype=jnp.float32), 'ln2_b': jnp.zeros((E,), dtype=jnp.float32)}
    _L0_ffn_all = _L0_ffn_setup()
    _L0_ffn_in = {k: v for k, v in _L0_ffn_all.items() if k in ('in_proj_w', 'in_proj_b', 'out_proj_w', 'out_proj_b', 'gate_w', 'gate_b', 'expert_w', 'expert_b', 'ln1_w', 'ln1_b', 'ln2_w', 'ln2_b')}
    del _L0_ffn_all
    return {'x': x, 'ctx_1024': ctx_1024, 'mask_Bx1xSxS2_bk1': mask_Bx1xSxS2_bk1, 'g_xattn': g_xattn, 'g_ffn': g_ffn, 'L0_xattn_Wq': _L0_xattn_in['Wq'], 'L0_xattn_bq': _L0_xattn_in['bq'], 'L0_xattn_Wk': _L0_xattn_in['Wk'], 'L0_xattn_bk': _L0_xattn_in['bk'], 'L0_xattn_Wv': _L0_xattn_in['Wv'], 'L0_xattn_bv': _L0_xattn_in['bv'], 'L0_xattn_Wo': _L0_xattn_in['Wo'], 'L0_xattn_bo': _L0_xattn_in['bo'], 'L0_ffn_in_proj_w': _L0_ffn_in['in_proj_w'], 'L0_ffn_in_proj_b': _L0_ffn_in['in_proj_b'], 'L0_ffn_out_proj_w': _L0_ffn_in['out_proj_w'], 'L0_ffn_out_proj_b': _L0_ffn_in['out_proj_b'], 'L0_ffn_gate_w': _L0_ffn_in['gate_w'], 'L0_ffn_gate_b': _L0_ffn_in['gate_b'], 'L0_ffn_expert_w': _L0_ffn_in['expert_w'], 'L0_ffn_expert_b': _L0_ffn_in['expert_b'], 'L0_ffn_ln1_w': _L0_ffn_in['ln1_w'], 'L0_ffn_ln1_b': _L0_ffn_in['ln1_b'], 'L0_ffn_ln2_w': _L0_ffn_in['ln2_w'], 'L0_ffn_ln2_b': _L0_ffn_in['ln2_b']}

def reference(x, ctx_1024, mask_Bx1xSxS2_bk1, g_xattn, g_ffn, L0_xattn_Wq, L0_xattn_bq, L0_xattn_Wk, L0_xattn_bk, L0_xattn_Wv, L0_xattn_bv, L0_xattn_Wo, L0_xattn_bo, L0_ffn_in_proj_w, L0_ffn_in_proj_b, L0_ffn_out_proj_w, L0_ffn_out_proj_b, L0_ffn_gate_w, L0_ffn_gate_b, L0_ffn_expert_w, L0_ffn_expert_b, L0_ffn_ln1_w, L0_ffn_ln1_b, L0_ffn_ln2_w, L0_ffn_ln2_b):
    import jax
    import jax.numpy as jnp

    def _L0_xattn_ref(query, key, value, mask, Wq, bq, Wk, bk, Wv, bv, Wo, bo):
        import jax, jax.numpy as jnp
        import numpy as np
        EMBED = 256
        HEADS = 16
        HEAD_DIM = EMBED // HEADS
        B, S = (4, 512)

        def _split_heads(x):
            b, s, _ = x.shape
            return x.reshape(b, s, HEADS, HEAD_DIM).transpose(0, 2, 1, 3)
        q = _split_heads(query @ Wq.T + bq)
        k = _split_heads(key @ Wk.T + bk)
        v = _split_heads(value @ Wv.T + bv)
        scores = jnp.einsum('bhqd,bhkd->bhqk', q, k) / jnp.sqrt(jnp.float32(HEAD_DIM))
        scores = jnp.where(mask, jnp.float32(-1000000000.0), scores)
        attn = jax.nn.softmax(scores, axis=-1)
        out = jnp.einsum('bhqk,bhkd->bhqd', attn, v)
        out = out.transpose(0, 2, 1, 3).reshape(out.shape[0], -1, EMBED)
        return out @ Wo.T + bo

    def _L0_ffn_ref(x, in_proj_w, in_proj_b, out_proj_w, out_proj_b, gate_w, gate_b, expert_w, expert_b, ln1_w, ln1_b, ln2_w, ln2_b):
        import jax, jax.numpy as jnp
        import numpy as np
        NUM_HEADS = 16
        TOP_K = 2
        ROPE_BASE = 10000.0
        LN_EPS = 1e-05

        def _rope_sin_cos(S, D, dtype):
            inv_freq = 1.0 / ROPE_BASE ** (jnp.arange(0, D, 2, dtype=jnp.float32) / D)
            freqs = jnp.arange(S, dtype=jnp.float32)[:, None] * inv_freq[None, :]
            sin = jnp.sin(freqs).astype(dtype)[None, :, None, :]
            cos = jnp.cos(freqs).astype(dtype)[None, :, None, :]
            return (sin, cos)

        def _apply_rope(x, sin, cos):
            x1, x2 = (x[..., 0::2], x[..., 1::2])
            r1 = x1 * cos - x2 * sin
            r2 = x1 * sin + x2 * cos
            return jnp.stack([r1, r2], axis=-1).reshape(x.shape)

        def _layer_norm(x, w, b):
            mu = jnp.mean(x, axis=-1, keepdims=True)
            var = jnp.mean(jnp.square(x - mu), axis=-1, keepdims=True)
            return (x - mu) * jax.lax.rsqrt(var + LN_EPS) * w + b
        B, S, E = x.shape
        H = NUM_HEADS
        D = E // H
        xh = x.reshape(B, S, H, D)
        sin, cos = _rope_sin_cos(S, D, x.dtype)
        q_in = _apply_rope(xh, sin, cos).reshape(B, S, E)
        k_in = q_in
        v_in = x
        Wq, Wk, Wv = jnp.split(in_proj_w, 3, axis=0)
        bq, bk, bv = jnp.split(in_proj_b, 3, axis=0)
        q = (q_in @ Wq.T + bq).reshape(B, S, H, D)
        k = (k_in @ Wk.T + bk).reshape(B, S, H, D)
        v = (v_in @ Wv.T + bv).reshape(B, S, H, D)
        scale = 1.0 / jnp.sqrt(jnp.asarray(D, dtype=x.dtype))
        scores = jnp.einsum('bqhd,bkhd->bhqk', q, k) * scale
        causal = jnp.tril(jnp.ones((S, S), dtype=bool))
        scores = jnp.where(causal[None, None], scores, jnp.asarray(-jnp.inf, dtype=scores.dtype))
        attn = jax.nn.softmax(scores, axis=-1)
        ctx = jnp.einsum('bhqk,bkhd->bqhd', attn, v).reshape(B, S, E)
        attn_out = ctx @ out_proj_w.T + out_proj_b
        x1 = _layer_norm(x + attn_out, ln1_w, ln1_b)
        gates = jax.nn.softmax(x1 @ gate_w.T + gate_b, axis=-1)
        _, top_idx = jax.lax.top_k(gates, TOP_K)
        top_gates = jnp.take_along_axis(gates, top_idx, axis=-1)
        expert_outputs = jnp.einsum('bsd,efd->bsef', x1, expert_w) + expert_b[None, None]
        sel = jnp.take_along_axis(expert_outputs, top_idx[..., None], axis=2)
        moe_out = jnp.sum(sel * top_gates[..., None], axis=2)
        return _layer_norm(x1 + moe_out, ln2_w, ln2_b)
    x = x + jnp.tanh(g_xattn[0]) * _L0_xattn_ref(_layernorm(x, axis=-1), ctx_1024, ctx_1024, mask_Bx1xSxS2_bk1, L0_xattn_Wq, L0_xattn_bq, L0_xattn_Wk, L0_xattn_bk, L0_xattn_Wv, L0_xattn_bv, L0_xattn_Wo, L0_xattn_bo)
    x = x + jnp.tanh(g_ffn[0]) * _L0_ffn_ref(_layernorm(x, axis=-1), L0_ffn_in_proj_w, L0_ffn_in_proj_b, L0_ffn_out_proj_w, L0_ffn_out_proj_b, L0_ffn_gate_w, L0_ffn_gate_b, L0_ffn_expert_w, L0_ffn_expert_b, L0_ffn_ln1_w, L0_ffn_ln1_b, L0_ffn_ln2_w, L0_ffn_ln2_b)
    return x

_drawn_inputs = setup_inputs


def setup_inputs(seed=0):
    import zlib

    import numpy as np

    out = dict(_drawn_inputs(seed))
    spreads = {'L0_xattn_bq': (0.0, 0.1),
     'L0_xattn_bk': (0.0, 0.1),
     'L0_xattn_bv': (0.0, 0.1),
     'L0_xattn_bo': (0.0, 0.1),
     'L0_ffn_in_proj_b': (0.0, 0.1),
     'L0_ffn_out_proj_b': (0.0, 0.1),
     'L0_ffn_gate_b': (0.0, 0.1),
     'L0_ffn_expert_b': (0.0, 0.1),
     'L0_ffn_ln1_w': (1.0, 0.2),
     'L0_ffn_ln1_b': (0.0, 0.1),
     'L0_ffn_ln2_w': (1.0, 0.2),
     'L0_ffn_ln2_b': (0.0, 0.1)}
    factors = {}
    for name, (base, spread) in spreads.items():
        noise = np.random.default_rng([zlib.crc32(name.encode()), seed]).standard_normal(out[name].shape)
        drawn = base * np.exp(spread * noise) if base else spread * noise
        out[name] = jnp.asarray(drawn.astype(out[name].dtype))
    for name, factor in factors.items():
        out[name] = (out[name] * factor).astype(out[name].dtype)
    return out
```

```python
from contextlib import ExitStack

import numpy as np

import concourse.bass as bass
from concourse import mybir

ALU = mybir.AluOpType
ACT = mybir.ActivationFunctionType
AXIS_X = mybir.AxisListType.X
F32 = mybir.dt.float32
F32R = mybir.dt.float32r
BF16 = mybir.dt.bfloat16

P = 128
EMBED = 256
HEADS = 16
HEAD_DIM = EMBED // HEADS
CHUNKS = EMBED // P
HEADS_PER_CHUNK = HEADS // CHUNKS
BANK = 512
GROUP = BANK // P
GROUPS = HEADS // GROUP
STRIP = 32
EXPERTS = 8
SCALE = HEAD_DIM ** -0.5
EPS = 1e-5
MASKED = -(2.0 ** 100)


class Steps:

    def __init__(self, nc, ctx):
        self.nc, self.ctx = nc, ctx
        self.stream = "setup"
        self.sems, self.count, self.done = {}, {}, {}

    def count_up(self, sem, name, tile, by):
        if sem not in self.sems:
            self.sems[sem] = self.ctx.enter_context(self.nc.semaphore("s_" + sem))
            self.count[sem] = 0
        self.count[sem] += by
        self.done[name, tile] = (sem, self.count[sem])
        return self.sems[sem]


class Queue:

    def __init__(self, steps, name):
        self.steps, self.name, self.items, self.seen = steps, name, [], {}

    def wait(self, *keys):
        need = {}
        for name, tile in keys:
            if tile >= 0:
                sem, value = self.steps.done[name, tile]
                need[sem] = max(need.get(sem, 0), value)
        for sem, value in need.items():
            if self.seen.get(sem, 0) < value:
                self.seen[sem] = value
                self.items.append(lambda eng, s=self.steps.sems[sem], v=value: eng.wait_ge(s, v))

    def do(self, call, name=None, tile=0):
        if name is None:
            self.items.append(call)
        else:
            sem = self.steps.count_up(f"{self.name}_{self.steps.stream}", name, tile, 1)
            self.items.append(lambda eng: call(eng).then_inc(sem, 1))

    def dma(self, call, name, tile=0):
        sem = self.steps.count_up(name, name, tile, 16)
        self.items.append(lambda eng: call(eng).then_inc(sem, 16))

    def emit(self, eng):
        for item in self.items:
            item(eng)


def build(nc, dram, out):
    tiles = out.shape[0]
    with ExitStack() as ctx:
        def sb(name, shape, dt=F32):
            return ctx.enter_context(nc.sbuf_tensor(name, shape, dt))

        steps = Steps(nc, ctx)
        sp, pe, act, dve, pool = (Queue(steps, n) for n in ("sp", "pe", "act", "dve", "pool"))

        x_in = [sb(f"x_in{i}", [P, EMBED]) for i in range(3)]
        ctx_t = [sb(f"ctx_t{i}", [P, CHUNKS, P]) for i in range(3)]
        mask_u8 = [sb(f"mask_u8{i}", [P, 2, P], mybir.dt.uint8) for i in range(3)]
        mask_add = [sb(f"mask_add{i}", [P, 2, P], BF16) for i in range(2)]
        causal_add = sb("causal_add", [P, 2, P], BF16)
        ident = sb("ident", [P, P])
        ident_bf = sb("ident_bf", [P, P], BF16)
        pick = sb("pick", [P, HEADS, P], BF16)
        head_rows = sb("head_rows", [P, HEADS_PER_CHUNK])
        lower_tri = sb("lower_tri", [P, EXPERTS, EXPERTS])
        rope_cos = sb("rope_cos", [P, EMBED])
        rope_sin = sb("rope_sin", [P, EMBED])
        neg_half = sb("neg_half", [P, 1])

        mats = ["Aq", "Ak", "Av", "Ao", "Bq", "Bk", "Bv", "Bo"]
        weight = {m: [sb(f"w_{m}{part}", [P, CHUNKS, EMBED], F32R) for part in "ab"] for m in mats}
        experts_w = [sb(f"w_experts{part}", [P, CHUNKS, EXPERTS * EMBED], F32R) for part in "ab"]
        gate_f = sb("gate_f", [P, CHUNKS, EXPERTS])
        gate_w = [sb(f"w_gate{part}", [P, CHUNKS, EXPERTS], F32R) for part in "ab"]
        stage = [sb(f"stage{i}", [P, CHUNKS, EMBED]) for i in range(3)]
        expert_bias = sb("expert_bias", [P, EMBED])
        rows = {n: sb(f"row_{n}", [P, EMBED]) for n in
                ("bv_A", "bo_A", "bv_B", "bo_B", "ln1_w", "ln1_b", "ln2_w", "ln2_b")}
        gate_bias = sb("gate_bias", [P, EXPERTS])
        cols = {n: sb(f"col_{n}", [P, CHUNKS]) for n in ("bq_A", "bk_A", "bq_B", "bk_B")}
        gains = sb("gains", [P, 2])
        tanh_gains = sb("tanh_gains", [P, 2])

        stats = {n: sb(f"stats_{n}", [P, 6]) for n in ("A", "B", "1", "2")}
        mean_var = {n: sb(f"mean_var_{n}", [P, 2]) for n in ("A", "B", "1", "2")}
        var_eps = {n: sb(f"var_eps_{n}", [P, 1]) for n in ("A", "B", "1", "2")}
        rstd = {n: sb(f"rstd_{n}", [P, 1]) for n in ("A", "B", "1", "2")}

        xn = sb("xn", [P, EMBED])
        yn = [sb(f"yn{i}", [P, EMBED]) for i in range(3)]
        roped = sb("roped", [P, EMBED])
        rope_tmp = sb("rope_tmp", [P, EMBED])
        u_n = sb("u_n", [P, EMBED])
        u_g = sb("u_g", [P, EMBED])
        u = [sb(f"u{i}", [P, EMBED]) for i in range(2)]
        x1 = [sb(f"x1_{i}", [P, EMBED]) for i in range(5)]
        base = {t: sb(f"base_{t}", [P, EMBED]) for t in "AB"}
        z = sb("z", [P, EMBED])

        def parts(name, cols_):
            return [sb(f"{name}_{part}", [P, cols_], F32R) for part in "ab"]

        xn_t, ctx_ab, rope_t, y_t, u_t = (parts(n, EMBED) for n in ("xn_t", "ctx_ab", "rope_t", "y_t", "u_t"))
        q_f = {t: sb(f"q_f{t}", [P, EMBED]) for t in "AB"}
        k_f = {t: sb(f"k_f{t}", [P, EMBED]) for t in "AB"}
        q_ab = {t: parts(f"q_{t}", EMBED) for t in "AB"}
        k_a = {t: sb(f"k_a{t}", [P, EMBED], F32R) for t in "AB"}
        k_b = {t: sb(f"k_b{t}", [P, EMBED]) for t in "AB"}
        keys = {t: [[sb(f"keys_{t}{part}{i}", [P, HEADS, P], F32R) for part in "ab"] for i in range(1)] for t in "AB"}
        values = {t: sb(f"values_{t}", [P, HEADS, STRIP]) for t in "AB"}
        neg_max = {t: sb(f"neg_max_{t}", [P, HEADS]) for t in "AB"}
        neg_max_bf = {t: sb(f"neg_max_bf_{t}", [P, P], BF16) for t in "AB"}
        neg_max_t = {t: sb(f"neg_max_t_{t}", [P, P], BF16) for t in "AB"}
        probs = {t: sb(f"probs_{t}", [P, HEADS, P]) for t in "AB"}
        o_raw = {t: sb(f"o_raw_{t}", [P, BANK]) for t in "AB"}
        inv_sum = {t: sb(f"inv_sum_{t}", [P, HEADS]) for t in "AB"}
        o_norm = {t: sb(f"o_norm_{t}", [P, EMBED]) for t in "AB"}
        o_t = {t: parts(f"o_t_{t}", EMBED) for t in "AB"}

        logits = sb("logits", [P, EXPERTS])
        gate_top = sb("gate_top", [P, EXPERTS])
        neg_top = sb("neg_top", [P, 1])
        gate_exp = sb("gate_exp", [P, EXPERTS])
        gate_sum = sb("gate_sum", [P, 1])
        gate_inv = sb("gate_inv", [P, 1])
        beats = sb("beats", [P, EXPERTS, EXPERTS])
        equals = sb("equals", [P, EXPERTS, EXPERTS])
        rank = sb("rank", [P, EXPERTS])
        chosen = sb("chosen", [P, EXPERTS])
        gates = sb("gates", [P, P])
        gates_t = sb("gates_t", [P, P])
        moe = [sb(f"moe{i}", [P, EMBED]) for i in range(2)]
        v_n = sb("v_n", [P, EMBED])
        v_g = sb("v_g", [P, EMBED])
        x1_b = sb("x1_b", [P, EMBED])
        y_out = [sb(f"y_out{i}", [P, EMBED]) for i in range(2)]

        banks = [ctx.enter_context(nc.psum_tensor(f"bank{i}", [P, BANK], F32)) for i in range(8)]
        score_banks, pv_bank = banks[0:GROUPS], banks[6]
        work_banks = [banks[4], banks[5], banks[7]]
        score_free = [[] for _ in range(GROUPS)]
        pv_free = []
        work_free = [[] for _ in work_banks]
        work_turn = [0]

        def take_work():
            n = work_turn[0] % len(work_banks)
            work_turn[0] += 1
            pe.wait(*work_free[n])
            return n, work_banks[n]

        def products(out_ap, left, right, first=True, last=True, check=False):
            calls = [(l, r) for (la, lb), (ra, rb) in zip(left, right) for l, r in ((la, ra), (la, rb), (lb, ra))]
            for n, (l, r) in enumerate(calls):
                fn = (lambda eng, l=l, r=r, s=first and n == 0, e=last and n == len(calls) - 1:
                      eng.matmul(out_ap, l, r, start=s, stop=e, skip_group_check=check))
                if n < len(calls) - 1:
                    pe.do(fn)
            return fn

        def chunk(pair, c):
            return tuple(x[:, c * P:(c + 1) * P] for x in pair)

        def by_head(ap):
            return ap.rearrange("p (h d) -> p h d", d=HEAD_DIM)

        def spread(ap, shape):
            return ap.to_broadcast(shape)

        def setup():
            def load(dst, src, name, tile=0):
                sp.dma(lambda eng: eng.dma_start(dst, src), name, tile)

            for dst, src, name in ((rope_cos, "rope_cos", "ld_cos"), (rope_sin, "rope_sin", "ld_sin"),
                                   (head_rows, "head_rows", "ld_head")):
                load(dst[:], dram[src], name)
            for n, (g) in enumerate(("g_xattn", "g_ffn")):
                load(gains[:, n:n + 1], spread(dram[g].rearrange("(a n) -> a n", a=1), [P, 1]), f"ld_gain{n}")
            with_bias = {"bq_A": dram["L0_xattn_bq"], "bk_A": dram["L0_xattn_bk"],
                         "bq_B": dram["L0_ffn_in_proj_b"][0:EMBED],
                         "bk_B": dram["L0_ffn_in_proj_b"][EMBED:2 * EMBED]}
            for n, src in with_bias.items():
                for c in range(CHUNKS):
                    load(cols[n][:, c:c + 1], src[c * P:(c + 1) * P].rearrange("(p a) -> p a", a=1), "ld_cols")
            row_src = {"bv_A": dram["L0_xattn_bv"], "bo_A": dram["L0_xattn_bo"],
                       "bv_B": dram["L0_ffn_in_proj_b"][2 * EMBED:3 * EMBED], "bo_B": dram["L0_ffn_out_proj_b"],
                       "ln1_w": dram["L0_ffn_ln1_w"], "ln1_b": dram["L0_ffn_ln1_b"],
                       "ln2_w": dram["L0_ffn_ln2_w"], "ln2_b": dram["L0_ffn_ln2_b"]}

            def split_weight(n, src, dst):
                slot = n % len(stage)
                if n >= len(stage):
                    sp.wait(("w_b", n - len(stage)))
                sp.dma(lambda eng: eng.dma_start(stage[slot][:], src.rearrange("(c p) n -> p c n", p=P)),
                      f"ld_w{slot}", n)
                act.wait((f"ld_w{slot}", n))
                act.do(lambda eng: eng.activation(dst[0], stage[slot][:], ACT.Copy), "w_a", n)
                pool.wait(("w_a", n))
                pool.do(lambda eng: eng.tensor_tensor(dst[1], stage[slot][:], dst[0].bitcast(F32), ALU.subtract),
                        "w_b", n)

            pool.do(lambda eng: eng.memset(ident[:], 0.0), "c_zero")
            pool.do(lambda eng: eng.memset(pick[:], 0.0), "c_zero")
            pool.do(lambda eng: eng.memset(causal_add[:], 0.0), "c_zero")
            pool.do(lambda eng: eng.memset(neg_half[:], -0.5), "c_zero")
            pool.do(lambda eng: eng.memset(lower_tri[:], 1.0), "c_zero")
            pool.do(lambda eng: eng.memset(expert_bias[:], 0.0), "c_zero")
            pool.wait(("c_zero", 0))
            pool.do(lambda eng: eng.affine_select(out=ident[:], in_=ident[:], compare_op=ALU.not_equal, fill=1.0,
                                                  base=0, pattern=[[-1, P]], channel_multiplier=1), "c_ident")
            for n in range(2):
                pool.do(lambda eng, n=n: eng.affine_select(out=pick[:], in_=pick[:], compare_op=ALU.not_equal,
                                                           fill=1.0, base=-n * HEADS, pattern=[[-1, HEADS], [0, P]],
                                                           channel_multiplier=1), "c_pick")
                pool.wait(("c_pick", 0))
            for n, sign in enumerate((1, -1)):
                pool.do(lambda eng, n=n, sign=sign: eng.affine_select(
                    out=causal_add[:, n, :], in_=causal_add[:, n, :], compare_op=ALU.is_ge, fill=MASKED,
                    base=0, pattern=[[-sign, P]], channel_multiplier=sign), "c_causal")
            pool.do(lambda eng: eng.affine_select(out=lower_tri[:], in_=lower_tri[:], compare_op=ALU.is_gt, fill=0.0,
                                                  base=0, pattern=[[1, EXPERTS], [-1, EXPERTS]],
                                                  channel_multiplier=0), "c_tri")
            for t in "AB":
                dve.do(lambda eng, t=t: eng.memset(values[t][:], 1.0), "c_dve")
                dve.do(lambda eng, t=t: eng.memset(neg_max_bf[t][:], 0.0), "c_dve")
            dve.do(lambda eng: eng.memset(gates[:], 0.0), "c_dve")
            dve.wait(("c_ident", 0), ("c_dve", 0))
            dve.do(lambda eng: eng.tensor_copy(ident_bf[:], ident[:]), "c_ident_bf")

            load_tile(0)
            names = {"Aq": "WqT", "Ak": "WkT", "Av": "WvT", "Ao": "WoT"}
            n = 0
            for m in ("Ak", "Av", "Aq", "Ao"):
                split_weight(n, dram[names[m]], [w[:] for w in weight[m]])
                n += 1
            load_tile(1)
            for m, src in zip(("Bq", "Bk", "Bv"), range(3)):
                split_weight(n, dram["in_projT"][:, src * EMBED:(src + 1) * EMBED], [w[:] for w in weight[m]])
                n += 1
            split_weight(n, dram["out_projT"], [w[:] for w in weight["Bo"]])
            n += 1
            for r, src in row_src.items():
                load(rows[r][:], spread(src.rearrange("(a n) -> a n", a=1), [P, EMBED]), "ld_rows")
            load(gate_bias[:], spread(dram["L0_ffn_gate_b"].rearrange("(a n) -> a n", a=1), [P, EXPERTS]), "ld_rows")
            load(gate_f[:], dram["gate_wT"].rearrange("(c p) n -> p c n", p=P), "ld_rows")
            sp.wait(("c_zero", 0))
            load(expert_bias[0:EXPERTS, :], dram["L0_ffn_expert_b"], "ld_eb")
            for e in range(EXPERTS):
                cut = slice(e * EMBED, (e + 1) * EMBED)
                split_weight(n, dram["expertsT"][:, cut], [w[:, :, cut] for w in experts_w])
                n += 1
            act.wait(("ld_gain0", 0), ("ld_gain1", 0))
            act.do(lambda eng: eng.activation(tanh_gains[:], gains[:], ACT.Tanh), "c_tanh")
            act.wait(("ld_cols", 0))
            for t in "AB":
                act.do(lambda eng, t=t: eng.activation(cols[f"bq_{t}"][:], cols[f"bq_{t}"][:], ACT.Copy, scale=SCALE),
                       "c_bq")
            act.wait(("ld_rows", 0))
            act.do(lambda eng: eng.activation(gate_w[0][:], gate_f[:], ACT.Copy), "w_gate_a")
            pool.wait(("w_gate_a", 0))
            pool.do(lambda eng: eng.tensor_tensor(gate_w[1][:], gate_f[:], gate_w[0][:].bitcast(F32), ALU.subtract),
                    "w_gate_b")
            pool.wait(("c_tanh", 0), ("ld_rows", 0))
            for r, g in (("bo_A", 0), ("ln2_w", 1), ("ln2_b", 1)):
                pool.do(lambda eng, r=r, g=g: eng.tensor_scalar(rows[r][:], rows[r][:], tanh_gains[:, g:g + 1], 1.0,
                                                                ALU.mult, ALU.mult), "c_fold")

        def load_tile(t):
            s = t % 3
            sp.wait(("A_base", t - 3), ("ctx_b", t - 3), ("mask", t - 3))
            sp.dma(lambda eng: eng.dma_start(x_in[s][:], dram["x"][t]), f"ld_x{s}", t)
            sp.dma(lambda eng: eng.dma_start(ctx_t[s][:], dram["ctxT"][t].rearrange("(c p) k -> p c k", p=P)),
                  f"ld_c{s}", t)
            sp.dma(lambda eng: eng.dma_start(mask_u8[s][:], dram["masks"][t].rearrange("m p k -> p m k")),
                  f"ld_m{s}", t)

        def norm(n, t, src, dst, ready, free, name):
            dve.wait(*ready)
            dve.do(lambda eng: eng.bn_stats(stats[n][:], src[:]), f"st_{n}", t)
            dve.wait((f"st_{n}", t), (f"rstd_{n}", t - 1))
            dve.do(lambda eng: eng.bn_aggr(mean_var[n][:], stats[n][:]), f"mv_{n}", t)
            pool.wait((f"mv_{n}", t))
            pool.do(lambda eng: eng.tensor_scalar(var_eps[n][:], mean_var[n][:, 1:2], EPS, 1.0, ALU.add, ALU.mult),
                    f"ve_{n}", t)
            pool.wait((f"ve_{n}", t), (name, t - 1))
            pool.do(lambda eng: eng.tensor_tensor(rstd[n][:], var_eps[n][:], neg_half[:], ALU.pow), f"rstd_{n}", t)
            dve.wait((f"rstd_{n}", t), *free)
            dve.do(lambda eng: eng.tensor_scalar(dst[:], src[:], mean_var[n][:, 0:1], rstd[n][:], ALU.subtract,
                                                 ALU.mult), name, t)

        def split_out(n_bank, src, dst, name, t, ready, free):
            act.wait(ready, *free)
            act.do(lambda eng: eng.activation(dst[0], src, ACT.Copy), name + "_a", t)
            dve.wait((name + "_a", t))
            dve.do(lambda eng: eng.tensor_tensor(dst[1], src, dst[0].bitcast(F32), ALU.subtract), name + "_b", t)
            work_free[n_bank] = [(name + "_b", t)]

        def transposed(src, dst, name, t, ready, free):
            n, bank = take_work()
            pe.wait(*ready, ("c_ident", 0))
            for c in range(CHUNKS):
                pe.do(lambda eng, c=c: eng.transpose(bank[:, c * P:(c + 1) * P], src[:, c * P:(c + 1) * P], ident[:]),
                      *((name + "_tp", t) if c == CHUNKS - 1 else ()))
            split_out(n, bank[:, 0:EMBED], [d[:] for d in dst], name, t, (name + "_tp", t), free)

        def prepare(t):
            s = t % 3
            norm("A", t, x_in[s], xn, [(f"ld_x{s}", t)], [("xn_tp", t - 1)], "xn")
            pool.wait((f"ld_c{s}", t), ("Av_mm", t - 1), ("Ak_mm", t - 1))
            pool.do(lambda eng: eng.tensor_copy(ctx_ab[0][:], ctx_t[s][:].rearrange("p c k -> p (c k)")), "ctx_a", t)
            pool.wait(("ctx_a", t))
            pool.do(lambda eng: eng.tensor_tensor(ctx_ab[1][:], ctx_t[s][:].rearrange("p c k -> p (c k)"),
                                                  ctx_ab[0][:].bitcast(F32), ALU.subtract), "ctx_b", t)
            pool.wait((f"ld_m{s}", t), ("A_st", t - 2))
            pool.do(lambda eng: eng.tensor_scalar(mask_add[t % 2][:], mask_u8[s][:], MASKED, 1.0, ALU.mult, ALU.mult),
                    "mask", t)

        def project_t(tag, what, t, src, ready, dst, scale, free):
            name = tag + what
            n, bank = take_work()
            pe.wait(*ready, ("w_b", order[name]))
            w = weight[name]
            for m in range(CHUNKS):
                last = products(bank[:, m * P:(m + 1) * P],
                                [tuple(x[:, c, m * P:(m + 1) * P] for x in w) for c in range(CHUNKS)],
                                [chunk(src, c) for c in range(CHUNKS)])
                pe.do(last, *((name + "_mm", t) if m == CHUNKS - 1 else ()))
            act.wait((name + "_mm", t), *free, ("c_bq", 0))
            for m in range(CHUNKS):
                act.do(lambda eng, m=m: eng.activation(dst[:, m * P:(m + 1) * P], bank[:, m * P:(m + 1) * P],
                                                       ACT.Identity, bias=cols[f"b{what}_{tag}"][:, m:m + 1],
                                                       scale=scale), name + "_f", t)
            work_free[n] = [(name + "_f", t)]

        def project_k(tag, t, src, ready):
            project_t(tag, "k", t, src, ready, k_f[tag], 1.0, [(tag + "_keys_a", t - 1), (tag + "_kb", t - 1)])
            pool.wait((tag + "k_f", t), (tag + "_kb", t - 1))
            pool.do(lambda eng: eng.tensor_copy(k_a[tag][:], k_f[tag][:]), tag + "_ka", t)
            pool.wait((tag + "_ka", t))
            pool.do(lambda eng: eng.tensor_tensor(k_b[tag][:], k_f[tag][:], k_a[tag][:].bitcast(F32), ALU.subtract),
                    tag + "_kb", t)
            for part, queue, src_k, ready_k in ((0, dve, k_f[tag], (tag + "k_f", t)),
                                                (1, pool, k_b[tag], (tag + "_kb", t))):
                queue.wait(ready_k, (tag + "_st", t - 1), ("ld_head", 0))
                for c in range(CHUNKS):
                    hs = slice(c * HEADS_PER_CHUNK, (c + 1) * HEADS_PER_CHUNK)
                    shape = [P, HEADS_PER_CHUNK, P]
                    queue.do(lambda eng, c=c, hs=hs, part=part, src_k=src_k: eng.tensor_tensor(
                        keys[tag][0][part][:, hs, :],
                        src_k[:, c * P:(c + 1) * P].unsqueeze(1).to_broadcast(shape),
                        head_rows[:].unsqueeze(2).to_broadcast(shape), ALU.mult),
                        f"{tag}_keys_{'ab'[part]}", t)

        def project_q(tag, t, src, ready):
            project_t(tag, "q", t, src, ready, q_f[tag], SCALE, [(tag + "_qb", t - 1)])
            pool.wait((tag + "q_f", t), (tag + "_st", t - 1))
            pool.do(lambda eng: eng.tensor_copy(q_ab[tag][0][:], q_f[tag][:]), tag + "_qa", t)
            pool.wait((tag + "_qa", t))
            pool.do(lambda eng: eng.tensor_tensor(q_ab[tag][1][:], q_f[tag][:], q_ab[tag][0][:].bitcast(F32),
                                                  ALU.subtract), tag + "_qb", t)

        def project_v(tag, t, src, ready):
            name = tag + "v"
            n, bank = take_work()
            pe.wait(*ready, ("w_b", order[name]))
            last = products(bank[:, 0:EMBED], [chunk(src, c) for c in range(CHUNKS)],
                            [tuple(w[:, c, :] for w in weight[name]) for c in range(CHUNKS)])
            pe.do(last, name + "_mm", t)
            dve.wait((name + "_mm", t), (tag + "_pv", t - 1), ("ld_rows", 0), ("c_dve", 0))
            dve.do(lambda eng: eng.tensor_tensor(values[tag][:, :, 0:HEAD_DIM], by_head(bank[:, 0:EMBED]),
                                                 by_head(rows["bv_" + tag][:]), ALU.add), tag + "_v", t)
            work_free[n] = [(tag + "_v", t)]

        def add_mask(g, add, stop):
            return lambda eng: eng.matmul(score_banks[g][:], ident_bf[:],
                                          add.unsqueeze(1).to_broadcast([P, GROUP, P]), start=True, stop=stop,
                                          skip_group_check=True)

        def scores(tag, t, mask, mask_ready):
            pe.wait((tag + "_qa", t), (tag + "_keys_a", t), *mask_ready, ("c_ident_bf", 0))
            for g in range(GROUPS):
                pe.wait(*score_free[g])
                pe.do(add_mask(g, mask[:, 0, :], False))
                c = g * GROUP // HEADS_PER_CHUNK
                pe.do(lambda eng, g=g, c=c: eng.matmul(score_banks[g][:], q_ab[tag][0][:, c * P:(c + 1) * P],
                                                       keys[tag][0][0][:, g * GROUP:(g + 1) * GROUP, :],
                                                       start=False, stop=True, skip_group_check=True),
                      f"{tag}_s{g}", t)
                dve.wait((f"{tag}_s{g}", t), (tag + "_nm", t - 1))
                dve.do(lambda eng, g=g: eng.tensor_reduce(
                    neg_max[tag][:, g * GROUP:(g + 1) * GROUP],
                    score_banks[g][:].rearrange("p (h k) -> p h k", k=P), AXIS_X, ALU.max, negate=True),
                    f"{tag}_max{g}", t)
                score_free[g] = [(f"{tag}_max{g}", t)]
            hi, lo = neg_max_bf[tag][:, 0:HEADS], neg_max_bf[tag][:, HEADS:2 * HEADS]
            dve.wait(*[(f"{tag}_max{g}", t) for g in range(GROUPS)], (tag + "_mt_tp", t - 1), ("c_dve", 0))
            dve.do(lambda eng: eng.tensor_copy(hi, neg_max[tag][:]), tag + "_nmh", t)
            dve.wait((tag + "_nmh", t))
            dve.do(lambda eng: eng.tensor_tensor(lo, neg_max[tag][:], hi, ALU.subtract), tag + "_nm", t)

        def scores_t(tag, t, mask):
            pe.wait((tag + "_qb", t), (tag + "_keys_b", t))
            ka, kb = keys[tag][0]
            for g in range(GROUPS):
                pe.wait(*score_free[g])
                pe.do(add_mask(g, mask[:, 1, :], False))
                for j in range(GROUP):
                    h = g * GROUP + j
                    q_parts = chunk(q_ab[tag], h // HEADS_PER_CHUNK)
                    pe.do(products(score_banks[g][:, j * P:(j + 1) * P], [(ka[:, h, :], kb[:, h, :])], [q_parts],
                                   first=False, last=False, check=True), *((tag + "_st", t) if h == HEADS - 1 else ()))

        def subtract_max(tag, t):
            n, bank = take_work()
            pe.wait((tag + "_nm", t), ("c_ident_bf", 0), ("c_pick", 0))
            pe.do(lambda eng: eng.transpose(bank[:, 0:P // 2].bitcast(BF16), neg_max_bf[tag][:], ident_bf[:]),
                  tag + "_mt_tp", t)
            act.wait((tag + "_mt_tp", t), (f"{tag}_sm{GROUPS - 1}", t - 1))
            act.do(lambda eng: eng.activation(neg_max_t[tag][:], bank[:, 0:P // 2].bitcast(BF16), ACT.Copy),
                   tag + "_mt", t)
            work_free[n] = [(tag + "_mt", t)]
            pe.wait((tag + "_mt", t))
            for g in range(GROUPS):
                for j in range(GROUP):
                    h = g * GROUP + j
                    pe.do(lambda eng, g=g, j=j, h=h: eng.matmul(
                        score_banks[g][:, j * P:(j + 1) * P], pick[:, h, :], neg_max_t[tag][:], start=False,
                        stop=True, skip_group_check=True), *((f"{tag}_sm{g}", t) if j == GROUP - 1 else ()))
                act.wait((f"{tag}_sm{g}", t), (tag + "_pv", t - 1))
                act.do(lambda eng, g=g: eng.activation(
                    probs[tag][:, g * GROUP:(g + 1) * GROUP, :].rearrange("p h q -> p (h q)"), score_banks[g][:],
                    ACT.Exp), f"{tag}_exp{g}", t)
                score_free[g] = [(f"{tag}_exp{g}", t)]

        def attend(tag, t):
            pe.wait((tag + "_v", t), *pv_free)
            for g in range(GROUPS):
                pe.wait((f"{tag}_exp{g}", t))
                for j in range(GROUP):
                    h = g * GROUP + j
                    pe.do(lambda eng, g=g, j=j, h=h: eng.matmul(
                        pv_bank[STRIP * j:STRIP * (j + 1), g * P:(g + 1) * P], values[tag][:, h, :],
                        probs[tag][:, h, :], start=True, stop=True, tile_position=(0, STRIP * j)),
                        *((tag + "_pv", t) if h == HEADS - 1 else ()))
            act.wait((tag + "_pv", t), (tag + "_or_tp", t - 1))
            act.do(lambda eng: eng.activation(o_raw[tag][:], pv_bank[:], ACT.Copy), tag + "_or", t)
            pv_free[:] = [(tag + "_or", t)]

        def normalise(tag, t):
            n, bank = take_work()
            pe.wait((tag + "_or", t))
            for g in range(GROUPS):
                pe.do(lambda eng, g=g: eng.transpose(bank[:, g * P:(g + 1) * P], o_raw[tag][:, g * P:(g + 1) * P],
                                                     ident[:]), *((tag + "_or_tp", t) if g == GROUPS - 1 else ()))
            heads = bank[:].rearrange("p (h s) -> p h s", s=STRIP)
            dve.wait((tag + "_or_tp", t), (tag + "_on", t - 1))
            dve.do(lambda eng: eng.reciprocal(inv_sum[tag][:].unsqueeze(2), heads[:, :, HEAD_DIM:HEAD_DIM + 1]),
                   tag + "_inv", t)
            dve.wait((tag + "_inv", t), (tag + "_ot_tp", t - 1))
            dve.do(lambda eng: eng.tensor_tensor(by_head(o_norm[tag][:]), heads[:, :, 0:HEAD_DIM],
                                                 inv_sum[tag][:].unsqueeze(2).to_broadcast([P, HEADS, HEAD_DIM]),
                                                 ALU.mult), tag + "_on", t)
            work_free[n] = [(tag + "_on", t)]

        def project_o(tag, t):
            transposed(o_norm[tag], o_t[tag], tag + "_ot", t, [(tag + "_on", t)], [(tag + "o_mm", t - 1)])
            n, bank = take_work()
            pe.wait((tag + "_ot_b", t), ("w_b", order[tag + "o"]))
            pe.do(products(bank[:, 0:EMBED], [chunk(o_t[tag], c) for c in range(CHUNKS)],
                           [tuple(w[:, c, :] for w in weight[tag + "o"]) for c in range(CHUNKS)]), tag + "o_mm", t)
            return n, bank

        def finish_a(t, n, bank):
            s = t % 3
            pool.wait((f"ld_x{s}", t), ("c_fold", 0), ("A_res", t - 1))
            pool.do(lambda eng: eng.tensor_tensor(base["A"][:], x_in[s][:], rows["bo_A"][:], ALU.add), "A_base", t)
            dve.wait(("Ao_mm", t), ("A_base", t), ("c_tanh", 0), ("x1_b", t - 5))
            dve.do(lambda eng: eng.scalar_tensor_tensor(out=x1[t % 5][:], in0=bank[:, 0:EMBED],
                                                        scalar=tanh_gains[:, 0:1], in1=base["A"][:], op0=ALU.mult,
                                                        op1=ALU.add), "A_res", t)
            work_free[n] = [("A_res", t)]
            y = yn[t % 3]
            norm("B", t, x1[t % 5], y, [("A_res", t)], [("B_base", t - 3), ("y_t_tp", t - 3), ("rope2", t - 3)], "yn")
            pairs = y[:].rearrange("p (n two) -> p n two", two=2)
            tmp = rope_tmp[:].rearrange("p (n two) -> p n two", two=2)
            sin = rope_sin[:].rearrange("p (n two) -> p n two", two=2)
            pool.wait(("yn", t), ("rope_t_tp", t - 1), ("ld_cos", 0), ("ld_sin", 0))
            pool.do(lambda eng: eng.tensor_tensor(roped[:], y[:], rope_cos[:], ALU.mult), "rope1", t)
            pool.wait(("rope3", t - 1))
            for n_ in range(2):
                pool.do(lambda eng, n_=n_: eng.tensor_tensor(tmp[:, :, n_:n_ + 1], pairs[:, :, 1 - n_:2 - n_],
                                                             sin[:, :, n_:n_ + 1], ALU.mult), "rope2", t)
            pool.wait(("rope1", t), ("rope2", t))
            pool.do(lambda eng: eng.tensor_tensor(roped[:], roped[:], rope_tmp[:], ALU.add), "rope3", t)

        def base_b(t):
            pool.wait(("yn", t), ("B_res", t - 1), ("ld_rows", 0))
            pool.do(lambda eng: eng.tensor_tensor(base["B"][:], yn[t % 3][:], rows["bo_B"][:], ALU.add), "B_base", t)

        def finish_b(t, n, bank):
            dve.wait(("Bo_mm", t), ("B_base", t), ("un", t - 1))
            dve.do(lambda eng: eng.tensor_tensor(z[:], bank[:, 0:EMBED], base["B"][:], ALU.add), "B_res", t)
            work_free[n] = [("B_res", t)]
            norm("1", t, z, u_n, [("B_res", t)], [("ug", t - 1)], "un")
            pool.wait(("un", t), ("ld_rows", 0), ("u", t - 1))
            pool.do(lambda eng: eng.tensor_tensor(u_g[:], u_n[:], rows["ln1_w"][:], ALU.mult), "ug", t)
            pool.wait(("ug", t), ("moe0", t - 2), ("u_t_tp", t - 2))
            pool.do(lambda eng: eng.tensor_tensor(u[t % 2][:], u_g[:], rows["ln1_b"][:], ALU.add), "u", t)

        def gate(t):
            n, bank = take_work()
            pe.wait(("u_t_b", t), ("w_gate_b", 0))
            pe.do(products(bank[:, 0:EXPERTS], [chunk(u_t, c) for c in range(CHUNKS)],
                           [tuple(w[:, c, :] for w in gate_w) for c in range(CHUNKS)]), "gate_mm", t)
            dve.wait(("gate_mm", t), ("ld_rows", 0), ("gate_exp", t - 1), ("chosen", t - 1))
            dve.do(lambda eng: eng.tensor_tensor(logits[:], bank[:, 0:EXPERTS], gate_bias[:], ALU.add), "logits", t)
            work_free[n] = [("logits", t)]
            dve.wait(("logits", t))
            dve.do(lambda eng: eng.tensor_reduce(neg_top[:], logits[:], AXIS_X, ALU.max, negate=True), "neg_top", t)
            act.wait(("neg_top", t), ("gates", t - 1))
            act.do(lambda eng: eng.activation(gate_exp[:], logits[:], ACT.Exp, bias=neg_top[:], accum_out=gate_sum[:]),
                   "gate_exp", t)
            other = logits[:].unsqueeze(1).to_broadcast([P, EXPERTS, EXPERTS])
            this = logits[:].unsqueeze(2).to_broadcast([P, EXPERTS, EXPERTS])
            dve.do(lambda eng: eng.tensor_tensor(beats[:], other, this, ALU.is_gt), "beats", t)
            dve.do(lambda eng: eng.tensor_tensor(equals[:], other, this, ALU.is_equal), "equals", t)
            dve.wait(("equals", t), ("c_tri", 0))
            dve.do(lambda eng: eng.tensor_tensor(equals[:], equals[:], lower_tri[:], ALU.mult), "equals_low", t)
            dve.wait(("equals_low", t), ("beats", t))
            dve.do(lambda eng: eng.tensor_tensor(beats[:], beats[:], equals[:], ALU.add), "beats_all", t)
            dve.wait(("beats_all", t))
            dve.do(lambda eng: eng.tensor_reduce(rank[:], beats[:], AXIS_X, ALU.add), "rank", t)
            dve.wait(("gate_exp", t))
            dve.do(lambda eng: eng.reciprocal(gate_inv[:], gate_sum[:]), "gate_inv", t)
            dve.wait(("rank", t))
            dve.do(lambda eng: eng.scalar_tensor_tensor(out=chosen[:], in0=rank[:], scalar=1.5, in1=gate_exp[:],
                                                        op0=ALU.is_lt, op1=ALU.mult), "chosen", t)
            dve.wait(("chosen", t), ("gate_inv", t), ("gates_tp", t - 1), ("moe8", t - 1), ("c_dve", 0))
            dve.do(lambda eng: eng.tensor_scalar(gates[:, 0:EXPERTS], chosen[:], gate_inv[:], None, ALU.mult),
                   "gates", t)

        def expert_bias_sum(t):
            n, bank = take_work()
            pe.wait(("gates", t))
            pe.do(lambda eng, bank=bank: eng.transpose(bank[:, 0:P], gates[:], ident[:]), "gates_tp", t)
            act.wait(("gates_tp", t), ("bias_mm", t - 1))
            act.do(lambda eng, bank=bank: eng.activation(gates_t[:], bank[:, 0:P], ACT.Copy), "gates_t", t)
            work_free[n] = [("gates_t", t)]
            n, bank = take_work()
            pe.wait(("gates_t", t), ("ld_eb", 0))
            pe.do(lambda eng: eng.matmul(bank[:, 0:EMBED], gates_t[:], expert_bias[:], start=True, stop=True),
                  "bias_mm", t)
            dve.wait(("bias_mm", t), ("u", t), ("vn", t - 1))
            dve.do(lambda eng: eng.tensor_tensor(moe[0][:], bank[:, 0:EMBED], u[t % 2][:], ALU.add), "moe0", t)
            work_free[n] = [("moe0", t)]

        def expert_pair(t, pair):
            n, bank = take_work()
            cut = slice(pair * 2 * EMBED, (pair + 1) * 2 * EMBED)
            pe.wait(("u_t_b", t), ("w_b", order["E"] + EXPERTS - 1))
            pe.do(products(bank[:], [chunk(u_t, c) for c in range(CHUNKS)],
                           [tuple(w[:, c, cut] for w in experts_w) for c in range(CHUNKS)]), f"e_mm{pair}", t)
            dve.wait((f"e_mm{pair}", t))
            for e in (2 * pair, 2 * pair + 1):
                dve.wait((f"moe{e}", t))
                dve.do(lambda eng, e=e: eng.scalar_tensor_tensor(
                    out=moe[(e + 1) % 2][:], in0=bank[:, (e % 2) * EMBED:(e % 2 + 1) * EMBED],
                    scalar=gates[:, e:e + 1], in1=moe[e % 2][:], op0=ALU.mult, op1=ALU.add), f"moe{e + 1}", t)
            work_free[n] = [(f"moe{2 * pair + 2}", t)]

        def finish(t):
            norm("2", t, moe[0], v_n, [("moe8", t)], [("vg", t - 1)], "vn")
            pool.wait(("vn", t), ("c_fold", 0), ("out", t - 1))
            pool.do(lambda eng: eng.tensor_tensor(x1_b[:], x1[t % 5][:], rows["ln2_b"][:], ALU.add), "x1_b", t)
            pool.do(lambda eng: eng.tensor_tensor(v_g[:], v_n[:], rows["ln2_w"][:], ALU.mult), "vg", t)
            pool.wait(("vg", t), ("x1_b", t), (f"store{t % 2}", t - 2))
            pool.do(lambda eng: eng.tensor_tensor(y_out[t % 2][:], v_g[:], x1_b[:], ALU.add), "out", t)
            sp.wait(("out", t))
            sp.dma(lambda eng: eng.dma_start(out[t], y_out[t % 2][:]), f"store{t % 2}", t)

        order = {m: n for n, m in enumerate(("Ak", "Av", "Aq", "Ao", "Bq", "Bk", "Bv", "Bo", "E"))}

        setup()
        steps.stream = "A"
        prepare(0)
        for it in range(tiles + 3):
            a, b, c, m = it, it - 1, it - 2, it - 3
            in_a, in_b, in_c, in_m = (0 <= t < tiles for t in (a, b, c, m))
            if it + 2 < tiles:
                load_tile(it + 2)
            if in_a:
                steps.stream = "A"
                project_k("A", a, ctx_ab, [("ctx_b", a)])
                project_v("A", a, ctx_ab, [("ctx_b", a)])
                transposed(xn, xn_t, "xn", a, [("xn", a)], [("Aq_mm", a - 1)])
                project_q("A", a, xn_t, [("xn_b", a)])
            if in_c:
                steps.stream = "B"
                attend("B", c)
            if in_b:
                steps.stream = "B"
                transposed(roped, rope_t, "rope_t", b, [("rope3", b)], [("Bk_mm", b - 1), ("Bq_mm", b - 1)])
                transposed(yn[b % 3], y_t, "y_t", b, [("yn", b)], [("Bv_mm", b - 1)])
            if in_c:
                steps.stream = "B"
                base_b(c)
                normalise("B", c)
            if in_m:
                steps.stream = "M"
                transposed(u[m % 2], u_t, "u_t", m, [("u", m)], [("e_mm3", m - 1)])
                gate(m)
            if in_b:
                steps.stream = "B"
                project_k("B", b, rope_t, [("rope_t_b", b)])
            if in_a:
                steps.stream = "A"
                scores("A", a, mask_add[a % 2], [("mask", a)])
            if in_b:
                steps.stream = "B"
                project_q("B", b, rope_t, [("rope_t_b", b)])
                project_v("B", b, y_t, [("y_t_b", b)])
            if in_c:
                steps.stream = "B"
                finish_b(c, *project_o("B", c))
            if in_a:
                steps.stream = "A"
                scores_t("A", a, mask_add[a % 2])
                subtract_max("A", a)
            if in_m:
                steps.stream = "M"
                expert_bias_sum(m)
                expert_pair(m, 0)
                expert_pair(m, 1)
            if it + 1 < tiles:
                steps.stream = "A"
                prepare(it + 1)
            if in_b:
                steps.stream = "B"
                scores("B", b, causal_add, [("c_causal", 0)])
            if in_a:
                steps.stream = "A"
                attend("A", a)
            if in_m:
                steps.stream = "M"
                expert_pair(m, 2)
            if in_a:
                steps.stream = "A"
                normalise("A", a)
            if in_b:
                steps.stream = "B"
                scores_t("B", b, causal_add)
                subtract_max("B", b)
            if in_m:
                steps.stream = "M"
                expert_pair(m, 3)
            if in_a:
                steps.stream = "A"
                finish_a(a, *project_o("A", a))
            if in_m:
                steps.stream = "M"
                finish(m)
        sp.wait(("store0", tiles - 2 + tiles % 2), ("store1", tiles - 1 - tiles % 2))

        block = ctx.enter_context(nc.Block())
        block.sync(sp.emit)
        block.tensor(pe.emit)
        block.scalar(act.emit)
        block.vector(dve.emit)
        block.gpsimd(pool.emit)


def constants():
    inv_freq = np.float32(1.0) / np.float32(10000.0) ** (
        np.arange(0, HEAD_DIM, 2, dtype=np.float32) / np.float32(HEAD_DIM))
    freqs = np.arange(P, dtype=np.float32)[:, None] * inv_freq[None, :]
    cos = np.tile(np.repeat(np.cos(freqs), 2, axis=1), (1, HEADS)).astype(np.float32)
    sin = np.stack([-np.sin(freqs), np.sin(freqs)], axis=-1).reshape(P, HEAD_DIM)
    sin = np.tile(sin, (1, HEADS)).astype(np.float32)
    head_rows = (np.arange(P)[:, None] // HEAD_DIM == np.arange(HEADS_PER_CHUNK)[None, :]).astype(np.float32)
    return {"rope_cos": cos, "rope_sin": sin, "head_rows": head_rows}


def kernel(**inputs):
    from concourse import bacc
    from concourse.bass_utils import run_bass_kernel_spmd

    a = {k: np.asarray(v) for k, v in inputs.items()}
    x = a["x"]
    mask = a["mask_Bx1xSxS2_bk1"][:, 0]
    arrays = {
        "x": x,
        "ctxT": a["ctx_1024"].transpose(0, 2, 1),
        "masks": np.stack([mask, mask.transpose(0, 2, 1)], axis=1),
        "WqT": a["L0_xattn_Wq"].T, "WkT": a["L0_xattn_Wk"].T, "WvT": a["L0_xattn_Wv"].T, "WoT": a["L0_xattn_Wo"].T,
        "in_projT": a["L0_ffn_in_proj_w"].T, "out_projT": a["L0_ffn_out_proj_w"].T, "gate_wT": a["L0_ffn_gate_w"].T,
        "expertsT": a["L0_ffn_expert_w"].transpose(2, 0, 1).reshape(EMBED, EXPERTS * EMBED),
    }
    for name in ("g_xattn", "g_ffn", "L0_xattn_bq", "L0_xattn_bk", "L0_xattn_bv", "L0_xattn_bo",
                 "L0_ffn_in_proj_b", "L0_ffn_out_proj_b", "L0_ffn_gate_b", "L0_ffn_expert_b",
                 "L0_ffn_ln1_w", "L0_ffn_ln1_b", "L0_ffn_ln2_w", "L0_ffn_ln2_b"):
        arrays[name] = a[name]
    arrays.update(constants())
    arrays = {k: np.ascontiguousarray(v) for k, v in arrays.items()}

    nc = bacc.Bacc("TRN2", target_bir_lowering=False, num_devices=1)
    dram = {k: nc.dram_tensor(f"in_{k}", v.shape, mybir.dt.from_np(v.dtype), kind="ExternalInput").ap()
            for k, v in arrays.items()}
    out = nc.dram_tensor("out", x.shape, F32, kind="ExternalOutput").ap()
    build(nc, dram, out)
    result = run_bass_kernel_spmd(nc, [{f"in_{k}": v for k, v in arrays.items()}], core_ids=[0])
    return result.results[0]["out"]
```

```python
from contextlib import ExitStack

import numpy as np

import concourse.bass as bass
from concourse import mybir

ALU = mybir.AluOpType
ACT = mybir.ActivationFunctionType
AXIS_X = mybir.AxisListType.X
F32 = mybir.dt.float32
F32R = mybir.dt.float32r
BF16 = mybir.dt.bfloat16

P = 128
EMBED = 256
HEADS = 16
HEAD_DIM = EMBED // HEADS
CHUNKS = EMBED // P
HEADS_PER_CHUNK = HEADS // CHUNKS
BANK = 512
GROUP = BANK // P
GROUPS = HEADS // GROUP
STRIP = 32
EXPERTS = 8
SCALE = HEAD_DIM ** -0.5
EPS = 1e-5
MASKED = -(2.0 ** 100)


class Steps:

    def __init__(self, nc, ctx):
        self.nc, self.ctx = nc, ctx
        self.stream = "setup"
        self.sems, self.count, self.done = {}, {}, {}

    def count_up(self, sem, name, tile, by):
        if sem not in self.sems:
            self.sems[sem] = self.ctx.enter_context(self.nc.semaphore("s_" + sem))
            self.count[sem] = 0
        self.count[sem] += by
        self.done[name, tile] = (sem, self.count[sem])
        return self.sems[sem]


class Queue:

    def __init__(self, steps, name):
        self.steps, self.name, self.items, self.seen = steps, name, [], {}

    def wait(self, *keys):
        need = {}
        for name, tile in keys:
            if tile >= 0:
                sem, value = self.steps.done[name, tile]
                need[sem] = max(need.get(sem, 0), value)
        for sem, value in need.items():
            if self.seen.get(sem, 0) < value:
                self.seen[sem] = value
                self.items.append(lambda eng, s=self.steps.sems[sem], v=value: eng.wait_ge(s, v))

    def do(self, call, name=None, tile=0):
        if name is None:
            self.items.append(call)
        else:
            sem = self.steps.count_up(f"{self.name}_{self.steps.stream}", name, tile, 1)
            self.items.append(lambda eng: call(eng).then_inc(sem, 1))

    def dma(self, call, name, tile=0):
        sem = self.steps.count_up(name, name, tile, 16)
        self.items.append(lambda eng: call(eng).then_inc(sem, 16))

    def emit(self, eng):
        for item in self.items:
            item(eng)


def build(nc, dram, out):
    tiles = out.shape[0]
    with ExitStack() as ctx:
        def sb(name, shape, dt=F32):
            return ctx.enter_context(nc.sbuf_tensor(name, shape, dt))

        steps = Steps(nc, ctx)
        sp, pe, act, dve, pool = (Queue(steps, n) for n in ("sp", "pe", "act", "dve", "pool"))

        x_in = [sb(f"x_in{i}", [P, EMBED]) for i in range(3)]
        ctx_t = [sb(f"ctx_t{i}", [P, CHUNKS, P]) for i in range(3)]
        mask_u8 = [sb(f"mask_u8{i}", [P, 2, P], mybir.dt.uint8) for i in range(3)]
        mask_add = [sb(f"mask_add{i}", [P, 2, P], BF16) for i in range(2)]
        causal_add = sb("causal_add", [P, 2, P], BF16)
        ident = sb("ident", [P, P])
        ident_bf = sb("ident_bf", [P, P], BF16)
        pick = sb("pick", [P, HEADS, P], BF16)
        head_rows = sb("head_rows", [P, HEADS_PER_CHUNK])
        lower_tri = sb("lower_tri", [P, EXPERTS, EXPERTS])
        rope_cos = sb("rope_cos", [P, EMBED])
        rope_sin = sb("rope_sin", [P, EMBED])
        neg_half = sb("neg_half", [P, 1])

        mats = ["Aq", "Ak", "Av", "Ao", "Bq", "Bk", "Bv", "Bo"]
        weight = {m: [sb(f"w_{m}{part}", [P, CHUNKS, EMBED], F32R) for part in "ab"] for m in mats}
        experts_w = [sb(f"w_experts{part}", [P, CHUNKS, EXPERTS * EMBED], F32R) for part in "ab"]
        gate_f = sb("gate_f", [P, CHUNKS, EXPERTS])
        gate_w = [sb(f"w_gate{part}", [P, CHUNKS, EXPERTS], F32R) for part in "ab"]
        w_stage = [sb(f"w_stage{i}", [P, CHUNKS, EMBED]) for i in range(3)]
        expert_bias = sb("expert_bias", [P, EMBED])
        rows = {n: sb(f"row_{n}", [P, EMBED]) for n in
                ("bv_A", "bo_A", "bv_B", "bo_B", "ln1_w", "ln1_b", "ln2_w", "ln2_b")}
        gate_bias = sb("gate_bias", [P, EXPERTS])
        cols = {n: sb(f"col_{n}", [P, CHUNKS]) for n in ("bq_A", "bk_A", "bq_B", "bk_B")}
        gains = sb("gains", [P, 2])
        tanh_gains = sb("tanh_gains", [P, 2])

        stats = {n: sb(f"stats_{n}", [P, 6]) for n in ("A", "B", "1", "2")}
        mean_var = {n: sb(f"mean_var_{n}", [P, 2]) for n in ("A", "B", "1", "2")}
        var_eps = {n: sb(f"var_eps_{n}", [P, 1]) for n in ("A", "B", "1", "2")}
        rstd = {n: sb(f"rstd_{n}", [P, 1]) for n in ("A", "B", "1", "2")}

        xn = sb("xn", [P, EMBED])
        yn = [sb(f"yn{i}", [P, EMBED]) for i in range(3)]
        roped = sb("roped", [P, EMBED])
        rope_tmp = sb("rope_tmp", [P, EMBED])
        u_n = sb("u_n", [P, EMBED])
        u_g = sb("u_g", [P, EMBED])
        u = [sb(f"u{i}", [P, EMBED]) for i in range(2)]
        x1 = [sb(f"x1_{i}", [P, EMBED]) for i in range(5)]
        base = {t: sb(f"base_{t}", [P, EMBED]) for t in "AB"}
        z = sb("z", [P, EMBED])

        def parts(name, cols_):
            return [sb(f"{name}_{part}", [P, cols_], F32R) for part in "ab"]

        xn_t, ctx_ab, rope_t, y_t, u_t = (parts(n, EMBED) for n in ("xn_t", "ctx_ab", "rope_t", "y_t", "u_t"))
        q_f = {t: sb(f"q_f{t}", [P, EMBED]) for t in "AB"}
        k_f = {t: sb(f"k_f{t}", [P, EMBED]) for t in "AB"}
        q_a = {t: sb(f"q_a{t}", [P, EMBED], F32R) for t in "AB"}
        q_b = {t: sb(f"q_b{t}", [P, EMBED]) for t in "AB"}
        k_ab = {t: parts(f"k_{t}", EMBED) for t in "AB"}
        queries = {t: [sb(f"queries_{t}{part}", [P, HEADS, P], F32R) for part in "ab"] for t in "AB"}
        values = {t: sb(f"values_{t}", [P, HEADS, STRIP]) for t in "AB"}
        neg_max = {t: sb(f"neg_max_{t}", [P, HEADS]) for t in "AB"}
        neg_max_bf = {t: sb(f"neg_max_bf_{t}", [P, P], BF16) for t in "AB"}
        neg_max_t = {t: sb(f"neg_max_t_{t}", [P, P], BF16) for t in "AB"}
        probs = {t: sb(f"probs_{t}", [P, HEADS, P]) for t in "AB"}
        o_raw = {t: sb(f"o_raw_{t}", [P, BANK]) for t in "AB"}
        inv_sum = {t: sb(f"inv_sum_{t}", [P, HEADS]) for t in "AB"}
        o_norm = {t: sb(f"o_norm_{t}", [P, EMBED]) for t in "AB"}
        o_t = {t: parts(f"o_t_{t}", EMBED) for t in "AB"}

        logits = sb("logits", [P, EXPERTS])
        gate_top = sb("gate_top", [P, EXPERTS])
        neg_top = sb("neg_top", [P, 1])
        gate_exp = sb("gate_exp", [P, EXPERTS])
        gate_sum = sb("gate_sum", [P, 1])
        gate_inv = sb("gate_inv", [P, 1])
        beats = sb("beats", [P, EXPERTS, EXPERTS])
        equals = sb("equals", [P, EXPERTS, EXPERTS])
        rank = sb("rank", [P, EXPERTS])
        chosen = sb("chosen", [P, EXPERTS])
        gates = sb("gates", [P, P])
        gates_t = sb("gates_t", [P, P])
        moe = [sb(f"moe{i}", [P, EMBED]) for i in range(2)]
        v_n = sb("v_n", [P, EMBED])
        v_g = sb("v_g", [P, EMBED])
        x1_b = sb("x1_b", [P, EMBED])
        y_out = [sb(f"y_out{i}", [P, EMBED]) for i in range(2)]

        banks = [ctx.enter_context(nc.psum_tensor(f"bank{i}", [P, BANK], F32)) for i in range(8)]
        score_banks, pv_bank = banks[0:GROUPS], banks[6]
        work_banks = [banks[4], banks[5], banks[7]]
        score_free = [[] for _ in range(GROUPS)]
        pv_free = []
        work_free = [[] for _ in work_banks]
        work_turn = [0]

        def take_work():
            n = work_turn[0] % len(work_banks)
            work_turn[0] += 1
            pe.wait(*work_free[n])
            return n, work_banks[n]

        def products(out_ap, left, right, first=True, last=True, check=False):
            calls = [(l, r) for (la, lb), (ra, rb) in zip(left, right) for l, r in ((la, ra), (la, rb), (lb, ra))]
            for n, (l, r) in enumerate(calls):
                fn = (lambda eng, l=l, r=r, s=first and n == 0, e=last and n == len(calls) - 1:
                      eng.matmul(out_ap, l, r, start=s, stop=e, skip_group_check=check))
                if n < len(calls) - 1:
                    pe.do(fn)
            return fn

        def chunk(pair, c):
            return tuple(x[:, c * P:(c + 1) * P] for x in pair)

        def by_head(ap):
            return ap.rearrange("p (h d) -> p h d", d=HEAD_DIM)

        def spread(ap, shape):
            return ap.to_broadcast(shape)

        order = {m: n for n, m in enumerate(("Ak", "Av", "Aq", "Ao", "Bq", "Bk", "Bv", "Bo", "E"))}

        def load(dst, src, name, tile=0):
            sp.dma(lambda eng: eng.dma_start(dst, src), name, tile)

        row_src = {"bv_A": dram["L0_xattn_bv"], "bo_A": dram["L0_xattn_bo"],
                   "bv_B": dram["L0_ffn_in_proj_b"][2 * EMBED:3 * EMBED], "bo_B": dram["L0_ffn_out_proj_b"],
                   "ln1_w": dram["L0_ffn_ln1_w"], "ln1_b": dram["L0_ffn_ln1_b"],
                   "ln2_w": dram["L0_ffn_ln2_w"], "ln2_b": dram["L0_ffn_ln2_b"]}

        def split_weight(n, src, dst):
            slot = n % len(w_stage)
            sp.wait(("w_b", n - len(w_stage)))
            load(w_stage[slot][:], src.rearrange("(c p) n -> p c n", p=P), f"ld_w{slot}", n)
            act.wait((f"ld_w{slot}", n))
            act.do(lambda eng: eng.activation(dst[0], w_stage[slot][:], ACT.Copy), "w_a", n)
            dve.wait(("w_a", n))
            dve.do(lambda eng: eng.tensor_tensor(dst[1], w_stage[slot][:], dst[0].bitcast(F32), ALU.subtract),
                   "w_b", n)

        def setup():
            load(head_rows[:], dram["head_rows"], "ld_head")
            with_bias = {"bq_A": dram["L0_xattn_bq"], "bk_A": dram["L0_xattn_bk"],
                         "bq_B": dram["L0_ffn_in_proj_b"][0:EMBED],
                         "bk_B": dram["L0_ffn_in_proj_b"][EMBED:2 * EMBED]}
            for n, src in with_bias.items():
                for c in range(CHUNKS):
                    load(cols[n][:, c:c + 1], src[c * P:(c + 1) * P].rearrange("(p a) -> p a", a=1), "ld_cols")

            pool.do(lambda eng: eng.memset(ident[:], 0.0), "c_zero")
            pool.do(lambda eng: eng.memset(neg_half[:], -0.5), "c_zero")
            pool.wait(("c_zero", 0))
            pool.do(lambda eng: eng.affine_select(out=ident[:], in_=ident[:], compare_op=ALU.not_equal, fill=1.0,
                                                  base=0, pattern=[[-1, P]], channel_multiplier=1), "c_ident")
            for t in "AB":
                dve.do(lambda eng, t=t: eng.memset(values[t][:], 1.0), "c_dve")
                dve.do(lambda eng, t=t: eng.memset(neg_max_bf[t][:], 0.0), "c_dve")
            dve.do(lambda eng: eng.memset(gates[:], 0.0), "c_dve")
            dve.wait(("c_ident", 0), ("c_dve", 0))
            dve.do(lambda eng: eng.tensor_copy(ident_bf[:], ident[:]), "c_ident_bf")
            act.wait(("ld_cols", 0))
            for t in "AB":
                act.do(lambda eng, t=t: eng.activation(cols[f"bq_{t}"][:], cols[f"bq_{t}"][:], ACT.Copy, scale=SCALE),
                       "c_bq")

        def setup_more():
            dve.do(lambda eng: eng.memset(queries["A"][1][:].bitcast(F32), 0.0), "c_zero_q")
            dve.do(lambda eng: eng.memset(queries["B"][1][:].bitcast(F32), 0.0), "c_zero_q")
            pool.do(lambda eng: eng.memset(pick[:], 0.0), "c_zero")
            pool.do(lambda eng: eng.memset(causal_add[:], 0.0), "c_zero")
            pool.do(lambda eng: eng.memset(lower_tri[:], 1.0), "c_zero")
            pool.do(lambda eng: eng.memset(expert_bias[:], 0.0), "c_zero")
            pool.wait(("c_zero", 0))
            for n in range(2):
                pool.do(lambda eng, n=n: eng.affine_select(out=pick[:], in_=pick[:], compare_op=ALU.not_equal,
                                                           fill=1.0, base=-n * HEADS, pattern=[[-1, HEADS], [0, P]],
                                                           channel_multiplier=1), "c_pick")
                pool.wait(("c_pick", 0))
            for n, sign in enumerate((1, -1)):
                pool.do(lambda eng, n=n, sign=sign: eng.affine_select(
                    out=causal_add[:, n, :], in_=causal_add[:, n, :], compare_op=ALU.is_ge, fill=MASKED,
                    base=0, pattern=[[-sign, P]], channel_multiplier=sign), "c_causal")
            pool.do(lambda eng: eng.affine_select(out=lower_tri[:], in_=lower_tri[:], compare_op=ALU.is_gt, fill=0.0,
                                                  base=0, pattern=[[1, EXPERTS], [-1, EXPERTS]],
                                                  channel_multiplier=0), "c_tri")
            for r, src in row_src.items():
                load(rows[r][:], spread(src.rearrange("(a n) -> a n", a=1), [P, EMBED]), "ld_rows")
            load(gate_bias[:], spread(dram["L0_ffn_gate_b"].rearrange("(a n) -> a n", a=1), [P, EXPERTS]), "ld_rows")
            load(gate_f[:], dram["gate_wT"].rearrange("(c p) n -> p c n", p=P), "ld_rows")
            load(rope_cos[:], dram["rope_cos"], "ld_cos")
            load(rope_sin[:], dram["rope_sin"], "ld_sin")
            for n, g in enumerate(("g_xattn", "g_ffn")):
                load(gains[:, n:n + 1], spread(dram[g].rearrange("(a n) -> a n", a=1), [P, 1]), f"ld_gain{n}")
            act.wait(("ld_gain0", 0), ("ld_gain1", 0))
            act.do(lambda eng: eng.activation(tanh_gains[:], gains[:], ACT.Tanh), "c_tanh")
            act.wait(("ld_rows", 0))
            act.do(lambda eng: eng.activation(gate_w[0][:], gate_f[:], ACT.Copy), "w_gate_a")
            pool.wait(("w_gate_a", 0))
            pool.do(lambda eng: eng.tensor_tensor(gate_w[1][:], gate_f[:], gate_w[0][:].bitcast(F32), ALU.subtract),
                    "w_gate_b")
            pool.wait(("c_tanh", 0), ("ld_rows", 0))
            for r, g in (("bo_A", 0), ("ln2_w", 1), ("ln2_b", 1)):
                pool.do(lambda eng, r=r, g=g: eng.tensor_scalar(rows[r][:], rows[r][:], tanh_gains[:, g:g + 1], 1.0,
                                                                ALU.mult, ALU.mult), "c_fold")

        def load_weights_a(names):
            for m in names:
                split_weight(order[m], dram[f"W{m[1]}T"], [w[:] for w in weight[m]])

        def load_weights_b():
            for m, src in zip(("Bq", "Bk", "Bv"), range(3)):
                split_weight(order[m], dram["in_projT"][:, src * EMBED:(src + 1) * EMBED], [w[:] for w in weight[m]])
            split_weight(order["Bo"], dram["out_projT"], [w[:] for w in weight["Bo"]])

        def load_experts():
            load(expert_bias[0:EXPERTS, :], dram["L0_ffn_expert_b"], "ld_eb")
            for e in range(EXPERTS):
                cut = slice(e * EMBED, (e + 1) * EMBED)
                split_weight(order["E"] + e, dram["expertsT"][:, cut], [w[:, :, cut] for w in experts_w])

        def load_tile(t):
            s = t % 3
            sp.wait(("A_base", t - 3), ("xn", t - 3), ("ctx_b", t - 3), ("mask", t - 3))
            sp.dma(lambda eng: eng.dma_start(x_in[s][:], dram["x"][t]), f"ld_x{s}", t)
            sp.dma(lambda eng: eng.dma_start(ctx_t[s][:], dram["ctxT"][t].rearrange("(c p) k -> p c k", p=P)),
                  f"ld_c{s}", t)
            sp.dma(lambda eng: eng.dma_start(mask_u8[s][:], dram["masks"][t].rearrange("m p k -> p m k")),
                  f"ld_m{s}", t)

        def norm(n, t, src, dst, ready, free, name):
            dve.wait(*ready)
            dve.do(lambda eng: eng.bn_stats(stats[n][:], src[:]), f"st_{n}", t)
            dve.wait((f"st_{n}", t), (f"rstd_{n}", t - 1))
            dve.do(lambda eng: eng.bn_aggr(mean_var[n][:], stats[n][:]), f"mv_{n}", t)
            pool.wait((f"mv_{n}", t))
            pool.do(lambda eng: eng.tensor_scalar(var_eps[n][:], mean_var[n][:, 1:2], EPS, 1.0, ALU.add, ALU.mult),
                    f"ve_{n}", t)
            pool.wait((f"ve_{n}", t), (name, t - 1))
            pool.do(lambda eng: eng.tensor_tensor(rstd[n][:], var_eps[n][:], neg_half[:], ALU.pow), f"rstd_{n}", t)
            dve.wait((f"rstd_{n}", t), *free)
            dve.do(lambda eng: eng.tensor_scalar(dst[:], src[:], mean_var[n][:, 0:1], rstd[n][:], ALU.subtract,
                                                 ALU.mult), name, t)

        def split_out(n_bank, src, dst, name, t, ready, free):
            act.wait(ready, *free)
            act.do(lambda eng: eng.activation(dst[0], src, ACT.Copy), name + "_a", t)
            dve.wait((name + "_a", t))
            dve.do(lambda eng: eng.tensor_tensor(dst[1], src, dst[0].bitcast(F32), ALU.subtract), name + "_b", t)
            work_free[n_bank] = [(name + "_b", t)]

        def transposed(src, dst, name, t, ready, free):
            n, bank = take_work()
            pe.wait(*ready, ("c_ident", 0))
            for c in range(CHUNKS):
                pe.do(lambda eng, c=c: eng.transpose(bank[:, c * P:(c + 1) * P], src[:, c * P:(c + 1) * P], ident[:]),
                      *((name + "_tp", t) if c == CHUNKS - 1 else ()))
            split_out(n, bank[:, 0:EMBED], [d[:] for d in dst], name, t, (name + "_tp", t), free)

        def prepare(t):
            s = t % 3
            norm("A", t, x_in[s], xn, [(f"ld_x{s}", t)], [("xn_tp", t - 1)], "xn")
            pool.wait((f"ld_c{s}", t), ("Av_mm", t - 1), ("Ak_mm", t - 1))
            pool.do(lambda eng: eng.tensor_copy(ctx_ab[0][:], ctx_t[s][:].rearrange("p c k -> p (c k)")), "ctx_a", t)
            pool.wait(("ctx_a", t))
            pool.do(lambda eng: eng.tensor_tensor(ctx_ab[1][:], ctx_t[s][:].rearrange("p c k -> p (c k)"),
                                                  ctx_ab[0][:].bitcast(F32), ALU.subtract), "ctx_b", t)
            pool.wait((f"ld_m{s}", t), ("A_st", t - 2))
            pool.do(lambda eng: eng.tensor_scalar(mask_add[t % 2][:], mask_u8[s][:], MASKED, 1.0, ALU.mult, ALU.mult),
                    "mask", t)

        def project_t(tag, what, t, src, ready, dst, dst_a, scale, free):
            name = tag + what
            n, bank = take_work()
            pe.wait(*ready, ("w_b", order[name]))
            w = weight[name]
            for m in range(CHUNKS):
                last = products(bank[:, m * P:(m + 1) * P],
                                [tuple(x[:, c, m * P:(m + 1) * P] for x in w) for c in range(CHUNKS)],
                                [chunk(src, c) for c in range(CHUNKS)])
                pe.do(last, *((name + "_mm", t) if m == CHUNKS - 1 else ()))
            act.wait((name + "_mm", t), *free, ("c_bq", 0))
            for out_t, step in ((dst, name + "_f"), (dst_a, name + "_a")):
                for m in range(CHUNKS):
                    act.do(lambda eng, m=m, out_t=out_t: eng.activation(
                        out_t[:, m * P:(m + 1) * P], bank[:, m * P:(m + 1) * P], ACT.Identity,
                        bias=cols[f"b{what}_{tag}"][:, m:m + 1], scale=scale), step, t)
            work_free[n] = [(name + "_a", t)]

        def project_k(tag, t, src, ready):
            project_t(tag, "k", t, src, ready, k_f[tag], k_ab[tag][0], 1.0, [(tag + "_st", t - 1)])
            pool.wait((tag + "k_a", t))
            pool.do(lambda eng: eng.tensor_tensor(k_ab[tag][1][:], k_f[tag][:], k_ab[tag][0][:].bitcast(F32),
                                                  ALU.subtract), tag + "_kb", t)

        def project_q(tag, t, src, ready):
            project_t(tag, "q", t, src, ready, q_f[tag], q_a[tag], SCALE,
                      [(tag + "_queries_a", t - 1), (tag + "_qb", t - 1)])
            dve.wait((tag + "q_f", t), (tag + "_st", t - 1), ("ld_head", 0))
            shape = [P, HEADS_PER_CHUNK, P]
            for c in range(CHUNKS):
                hs = slice(c * HEADS_PER_CHUNK, (c + 1) * HEADS_PER_CHUNK)
                dve.do(lambda eng, c=c, hs=hs: eng.tensor_tensor(
                    queries[tag][0][:, hs, :], q_f[tag][:, c * P:(c + 1) * P].unsqueeze(1).to_broadcast(shape),
                    head_rows[:].unsqueeze(2).to_broadcast(shape), ALU.mult), f"{tag}_queries_a", t)
            pool.wait((tag + "q_a", t), (tag + "_queries_b", t - 1))
            pool.do(lambda eng: eng.tensor_tensor(q_b[tag][:], q_f[tag][:], q_a[tag][:].bitcast(F32), ALU.subtract),
                    tag + "_qb", t)

        def spread_queries_b(tag, t):
            act.wait((tag + "_qb", t), (tag + "_st", t - 1), ("c_zero_q", 0), ("ld_head", 0))
            for h in range(HEADS_PER_CHUNK):
                row = h * HEAD_DIM // STRIP * STRIP
                act.do(lambda eng, h=h, row=row: eng.activation(
                    queries[tag][1][row:row + STRIP, h::HEADS_PER_CHUNK, :],
                    q_b[tag][row:row + STRIP, :].rearrange("p (c q) -> p c q", c=CHUNKS), ACT.Copy,
                    scale=head_rows[row:row + STRIP, h:h + 1]), tag + "_queries_b", t)

        def project_v(tag, t, src, ready):
            name = tag + "v"
            n, bank = take_work()
            pe.wait(*ready, ("w_b", order[name]))
            last = products(bank[:, 0:EMBED], [chunk(src, c) for c in range(CHUNKS)],
                            [tuple(w[:, c, :] for w in weight[name]) for c in range(CHUNKS)])
            pe.do(last, name + "_mm", t)
            dve.wait((name + "_mm", t), (tag + "_pv", t - 1), ("ld_rows", 0), ("c_dve", 0))
            dve.do(lambda eng: eng.tensor_tensor(values[tag][:, :, 0:HEAD_DIM], by_head(bank[:, 0:EMBED]),
                                                 by_head(rows["bv_" + tag][:]), ALU.add), tag + "_v", t)
            work_free[n] = [(tag + "_v", t)]

        def add_mask(g, add, stop):
            return lambda eng: eng.matmul(score_banks[g][:], ident_bf[:],
                                          add.unsqueeze(1).to_broadcast([P, GROUP, P]), start=True, stop=stop,
                                          skip_group_check=True)

        def scores(tag, t, mask, mask_ready):
            pe.wait((tag + "k_a", t), (tag + "_queries_a", t), *mask_ready, ("c_ident_bf", 0))
            for g in range(GROUPS):
                pe.wait(*score_free[g])
                pe.do(add_mask(g, mask[:, 0, :], False))
                for j in range(GROUP):
                    h = g * GROUP + j
                    c = h // HEADS_PER_CHUNK
                    pe.do(lambda eng, g=g, j=j, h=h, c=c: eng.matmul(
                        score_banks[g][:, j * P:(j + 1) * P], queries[tag][0][:, h, :],
                        k_ab[tag][0][:, c * P:(c + 1) * P], start=False, stop=True, skip_group_check=True),
                        *((f"{tag}_s{g}", t) if j == GROUP - 1 else ()))
                dve.wait((f"{tag}_s{g}", t), (tag + "_nm", t - 1))
                dve.do(lambda eng, g=g: eng.tensor_reduce(
                    neg_max[tag][:, g * GROUP:(g + 1) * GROUP],
                    score_banks[g][:].rearrange("p (h k) -> p h k", k=P), AXIS_X, ALU.max, negate=True),
                    f"{tag}_max{g}", t)
                score_free[g] = [(f"{tag}_max{g}", t)]
            hi, lo = neg_max_bf[tag][:, 0:HEADS], neg_max_bf[tag][:, HEADS:2 * HEADS]
            dve.wait(*[(f"{tag}_max{g}", t) for g in range(GROUPS)], (tag + "_mt_tp", t - 1), ("c_dve", 0))
            dve.do(lambda eng: eng.tensor_copy(hi, neg_max[tag][:]), tag + "_nmh", t)
            dve.wait((tag + "_nmh", t))
            dve.do(lambda eng: eng.tensor_tensor(lo, neg_max[tag][:], hi, ALU.subtract), tag + "_nm", t)

        def scores_t(tag, t, mask):
            pe.wait((tag + "_kb", t), (tag + "_queries_b", t))
            q_ap = [q[:].rearrange("p h q -> p (h q)") for q in queries[tag]]
            for g in range(GROUPS):
                if g == GROUPS - 1:
                    transpose_max(tag, t)
                pe.wait(*score_free[g])
                pe.do(add_mask(g, mask[:, 1, :], False))
                pe.do(products(score_banks[g][:], [chunk(k_ab[tag], g * GROUP // HEADS_PER_CHUNK)],
                               [tuple(q[:, g * BANK:(g + 1) * BANK] for q in q_ap)],
                               first=False, last=False, check=True), *((tag + "_st", t) if g == GROUPS - 1 else ()))
            pe.wait((tag + "_mt", t))
            for g in range(GROUPS):
                for j in range(GROUP):
                    h = g * GROUP + j
                    pe.do(lambda eng, g=g, j=j, h=h: eng.matmul(
                        score_banks[g][:, j * P:(j + 1) * P], pick[:, h, :], neg_max_t[tag][:], start=False,
                        stop=True, skip_group_check=True), *((f"{tag}_sm{g}", t) if j == GROUP - 1 else ()))
                act.wait((f"{tag}_sm{g}", t), (tag + "_pv", t - 1))
                act.do(lambda eng, g=g: eng.activation(
                    probs[tag][:, g * GROUP:(g + 1) * GROUP, :].rearrange("p h q -> p (h q)"), score_banks[g][:],
                    ACT.Exp), f"{tag}_exp{g}", t)
                score_free[g] = [(f"{tag}_exp{g}", t)]

        def transpose_max(tag, t):
            n, bank = take_work()
            pe.wait((tag + "_nm", t), ("c_ident_bf", 0), ("c_pick", 0))
            pe.do(lambda eng: eng.transpose(bank[:, 0:P // 2].bitcast(BF16), neg_max_bf[tag][:], ident_bf[:]),
                  tag + "_mt_tp", t)
            act.wait((tag + "_mt_tp", t), (f"{tag}_sm{GROUPS - 1}", t - 1))
            act.do(lambda eng: eng.activation(neg_max_t[tag][:], bank[:, 0:P // 2].bitcast(BF16), ACT.Copy),
                   tag + "_mt", t)
            work_free[n] = [(tag + "_mt", t)]

        def attend(tag, t):
            pe.wait((tag + "_v", t), *pv_free)
            for g in range(GROUPS):
                pe.wait((f"{tag}_exp{g}", t))
                for j in range(GROUP):
                    h = g * GROUP + j
                    pe.do(lambda eng, g=g, j=j, h=h: eng.matmul(
                        pv_bank[STRIP * j:STRIP * (j + 1), g * P:(g + 1) * P], values[tag][:, h, :],
                        probs[tag][:, h, :], start=True, stop=True, tile_position=(0, STRIP * j)),
                        *((tag + "_pv", t) if h == HEADS - 1 else ()))
            act.wait((tag + "_pv", t), (tag + "_or_tp", t - 1))
            act.do(lambda eng: eng.activation(o_raw[tag][:], pv_bank[:], ACT.Copy), tag + "_or", t)
            pv_free[:] = [(tag + "_or", t)]

        def normalise(tag, t):
            n, bank = take_work()
            pe.wait((tag + "_or", t))
            for g in range(GROUPS):
                pe.do(lambda eng, g=g: eng.transpose(bank[:, g * P:(g + 1) * P], o_raw[tag][:, g * P:(g + 1) * P],
                                                     ident[:]), *((tag + "_or_tp", t) if g == GROUPS - 1 else ()))
            heads = bank[:].rearrange("p (h s) -> p h s", s=STRIP)
            dve.wait((tag + "_or_tp", t), (tag + "_on", t - 1))
            dve.do(lambda eng: eng.reciprocal(inv_sum[tag][:].unsqueeze(2), heads[:, :, HEAD_DIM:HEAD_DIM + 1]),
                   tag + "_inv", t)
            dve.wait((tag + "_inv", t), (tag + "_ot_tp", t - 1))
            dve.do(lambda eng: eng.tensor_tensor(by_head(o_norm[tag][:]), heads[:, :, 0:HEAD_DIM],
                                                 inv_sum[tag][:].unsqueeze(2).to_broadcast([P, HEADS, HEAD_DIM]),
                                                 ALU.mult), tag + "_on", t)
            work_free[n] = [(tag + "_on", t)]

        def transpose_o(tag, t):
            transposed(o_norm[tag], o_t[tag], tag + "_ot", t, [(tag + "_on", t)], [(tag + "o_mm", t - 1)])

        def project_o(tag, t):
            n, bank = take_work()
            pe.wait((tag + "_ot_b", t), ("w_b", order[tag + "o"]))
            pe.do(products(bank[:, 0:EMBED], [chunk(o_t[tag], c) for c in range(CHUNKS)],
                           [tuple(w[:, c, :] for w in weight[tag + "o"]) for c in range(CHUNKS)]), tag + "o_mm", t)
            return n, bank

        def finish_a(t, n, bank):
            dve.wait(("Ao_mm", t), ("A_base", t), ("c_tanh", 0), ("x1_b", t - 5))
            dve.do(lambda eng: eng.scalar_tensor_tensor(out=x1[t % 5][:], in0=bank[:, 0:EMBED],
                                                        scalar=tanh_gains[:, 0:1], in1=base["A"][:], op0=ALU.mult,
                                                        op1=ALU.add), "A_res", t)
            work_free[n] = [("A_res", t)]
            y = yn[t % 3]
            norm("B", t, x1[t % 5], y, [("A_res", t)], [("B_base", t - 3), ("y_t_tp", t - 3), ("rope2", t - 3)], "yn")
            pairs = y[:].rearrange("p (n two) -> p n two", two=2)
            tmp = rope_tmp[:].rearrange("p (n two) -> p n two", two=2)
            sin = rope_sin[:].rearrange("p (n two) -> p n two", two=2)
            pool.wait(("yn", t), ("rope_t_tp", t - 1), ("ld_cos", 0), ("ld_sin", 0))
            pool.do(lambda eng: eng.tensor_tensor(roped[:], y[:], rope_cos[:], ALU.mult), "rope1", t)
            pool.wait(("rope3", t - 1))
            for n_ in range(2):
                pool.do(lambda eng, n_=n_: eng.tensor_tensor(tmp[:, :, n_:n_ + 1], pairs[:, :, 1 - n_:2 - n_],
                                                             sin[:, :, n_:n_ + 1], ALU.mult), "rope2", t)
            pool.wait(("rope1", t), ("rope2", t))
            pool.do(lambda eng: eng.tensor_tensor(roped[:], roped[:], rope_tmp[:], ALU.add), "rope3", t)

        def base_a(t):
            s = t % 3
            pool.wait((f"ld_x{s}", t), ("c_fold", 0), ("A_res", t - 1))
            pool.do(lambda eng: eng.tensor_tensor(base["A"][:], x_in[s][:], rows["bo_A"][:], ALU.add), "A_base", t)

        def base_b(t):
            pool.wait(("yn", t), ("B_res", t - 1), ("ld_rows", 0))
            pool.do(lambda eng: eng.tensor_tensor(base["B"][:], yn[t % 3][:], rows["bo_B"][:], ALU.add), "B_base", t)

        def finish_b(t, n, bank):
            dve.wait(("Bo_mm", t), ("B_base", t), ("un", t - 1))
            dve.do(lambda eng: eng.tensor_tensor(z[:], bank[:, 0:EMBED], base["B"][:], ALU.add), "B_res", t)
            work_free[n] = [("B_res", t)]
            norm("1", t, z, u_n, [("B_res", t)], [("ug", t - 1)], "un")
            pool.wait(("un", t), ("ld_rows", 0), ("u", t - 1))
            pool.do(lambda eng: eng.tensor_tensor(u_g[:], u_n[:], rows["ln1_w"][:], ALU.mult), "ug", t)
            pool.wait(("ug", t), ("moe0", t - 2), ("u_t_tp", t - 2))
            pool.do(lambda eng: eng.tensor_tensor(u[t % 2][:], u_g[:], rows["ln1_b"][:], ALU.add), "u", t)

        def gate(t):
            n, bank = take_work()
            pe.wait(("u_t_b", t), ("w_gate_b", 0))
            pe.do(products(bank[:, 0:EXPERTS], [chunk(u_t, c) for c in range(CHUNKS)],
                           [tuple(w[:, c, :] for w in gate_w) for c in range(CHUNKS)]), "gate_mm", t)
            dve.wait(("gate_mm", t), ("ld_rows", 0), ("gate_exp", t - 1), ("chosen", t - 1))
            dve.do(lambda eng: eng.tensor_tensor(logits[:], bank[:, 0:EXPERTS], gate_bias[:], ALU.add), "logits", t)
            work_free[n] = [("logits", t)]
            dve.wait(("logits", t))
            dve.do(lambda eng: eng.tensor_reduce(neg_top[:], logits[:], AXIS_X, ALU.max, negate=True), "neg_top", t)
            act.wait(("neg_top", t), ("gates", t - 1))
            act.do(lambda eng: eng.activation(gate_exp[:], logits[:], ACT.Exp, bias=neg_top[:], accum_out=gate_sum[:]),
                   "gate_exp", t)
            other = logits[:].unsqueeze(1).to_broadcast([P, EXPERTS, EXPERTS])
            this = logits[:].unsqueeze(2).to_broadcast([P, EXPERTS, EXPERTS])
            dve.do(lambda eng: eng.tensor_tensor(beats[:], other, this, ALU.is_gt), "beats", t)
            dve.do(lambda eng: eng.tensor_tensor(equals[:], other, this, ALU.is_equal), "equals", t)
            dve.wait(("equals", t), ("c_tri", 0))
            dve.do(lambda eng: eng.tensor_tensor(equals[:], equals[:], lower_tri[:], ALU.mult), "equals_low", t)
            dve.wait(("equals_low", t), ("beats", t))
            dve.do(lambda eng: eng.tensor_tensor(beats[:], beats[:], equals[:], ALU.add), "beats_all", t)
            dve.wait(("beats_all", t))
            dve.do(lambda eng: eng.tensor_reduce(rank[:], beats[:], AXIS_X, ALU.add), "rank", t)
            dve.wait(("gate_exp", t))
            dve.do(lambda eng: eng.reciprocal(gate_inv[:], gate_sum[:]), "gate_inv", t)
            dve.wait(("rank", t))
            dve.do(lambda eng: eng.scalar_tensor_tensor(out=chosen[:], in0=rank[:], scalar=1.5, in1=gate_exp[:],
                                                        op0=ALU.is_lt, op1=ALU.mult), "chosen", t)
            dve.wait(("chosen", t), ("gate_inv", t), ("gates_tp", t - 1), ("moe8", t - 1), ("c_dve", 0))
            dve.do(lambda eng: eng.tensor_scalar(gates[:, 0:EXPERTS], chosen[:], gate_inv[:], None, ALU.mult),
                   "gates", t)

        def transpose_gates(t):
            n, bank = take_work()
            pe.wait(("gates", t))
            pe.do(lambda eng, bank=bank: eng.transpose(bank[:, 0:P], gates[:], ident[:]), "gates_tp", t)
            act.wait(("gates_tp", t), ("bias_mm", t - 1))
            act.do(lambda eng, bank=bank: eng.activation(gates_t[:], bank[:, 0:P], ACT.Copy), "gates_t", t)
            work_free[n] = [("gates_t", t)]

        def expert_bias_sum(t):
            n, bank = take_work()
            pe.wait(("gates_t", t), ("ld_eb", 0))
            pe.do(lambda eng: eng.matmul(bank[:, 0:EMBED], gates_t[:], expert_bias[:], start=True, stop=True),
                  "bias_mm", t)
            dve.wait(("bias_mm", t), ("u", t), ("vn", t - 1))
            dve.do(lambda eng: eng.tensor_tensor(moe[0][:], bank[:, 0:EMBED], u[t % 2][:], ALU.add), "moe0", t)
            work_free[n] = [("moe0", t)]

        def expert_pair(t, pair):
            n, bank = take_work()
            cut = slice(pair * 2 * EMBED, (pair + 1) * 2 * EMBED)
            pe.wait(("u_t_b", t), ("w_b", order["E"] + EXPERTS - 1))
            pe.do(products(bank[:], [chunk(u_t, c) for c in range(CHUNKS)],
                           [tuple(w[:, c, cut] for w in experts_w) for c in range(CHUNKS)]), f"e_mm{pair}", t)
            dve.wait((f"e_mm{pair}", t))
            for e in (2 * pair, 2 * pair + 1):
                dve.wait((f"moe{e}", t))
                dve.do(lambda eng, e=e: eng.scalar_tensor_tensor(
                    out=moe[(e + 1) % 2][:], in0=bank[:, (e % 2) * EMBED:(e % 2 + 1) * EMBED],
                    scalar=gates[:, e:e + 1], in1=moe[e % 2][:], op0=ALU.mult, op1=ALU.add), f"moe{e + 1}", t)
            work_free[n] = [(f"moe{2 * pair + 2}", t)]

        def finish(t):
            norm("2", t, moe[0], v_n, [("moe8", t)], [("vg", t - 1)], "vn")
            pool.wait(("vn", t), ("c_fold", 0), ("out", t - 1))
            pool.do(lambda eng: eng.tensor_tensor(x1_b[:], x1[t % 5][:], rows["ln2_b"][:], ALU.add), "x1_b", t)
            pool.do(lambda eng: eng.tensor_tensor(v_g[:], v_n[:], rows["ln2_w"][:], ALU.mult), "vg", t)
            pool.wait(("vg", t), ("x1_b", t), (f"store{t % 2}", t - 2))
            pool.do(lambda eng: eng.tensor_tensor(y_out[t % 2][:], v_g[:], x1_b[:], ALU.add), "out", t)
            sp.wait(("out", t))
            sp.dma(lambda eng: eng.dma_start(out[t], y_out[t % 2][:]), f"store{t % 2}", t)

        load_tile(0)
        setup()
        load_weights_a(("Ak", "Av", "Aq"))
        steps.stream = "A"
        prepare(0)
        steps.stream = "setup"
        load_tile(1)
        load_weights_a(("Ao",))
        setup_more()
        for it in range(tiles + 3):
            a, b, c, m = it, it - 1, it - 2, it - 3
            active = {"a": a < tiles, "b": 0 <= b < tiles, "c": 0 <= c < tiles, "m": 0 <= m < tiles}
            stream_of = {"a": "A", "b": "B", "c": "B", "m": "M", "n": "M"}
            active["n"] = active["c"]

            def stage(who, call, *args):
                if active[who]:
                    steps.stream = stream_of[who]
                    call(*args)

            if it + 2 < tiles:
                load_tile(it + 2)
            stage("a", transposed, xn, xn_t, "xn", a, [("xn", a)], [("Aq_mm", a - 1)])
            stage("a", project_k, "A", a, ctx_ab, [("ctx_b", a)])
            stage("a", project_q, "A", a, xn_t, [("xn_b", a)])
            stage("a", project_v, "A", a, ctx_ab, [("ctx_b", a)])
            stage("a", base_a, a)
            stage("c", base_b, c)
            stage("c", attend, "B", c)
            stage("b", transposed, roped, rope_t, "rope_t", b, [("rope3", b)], [("Bk_mm", b - 1), ("Bq_mm", b - 1)])
            stage("b", transposed, yn[b % 3], y_t, "y_t", b, [("yn", b)], [("Bv_mm", b - 1)])
            stage("a", spread_queries_b, "A", a)
            stage("m", expert_pair, m, 0)
            stage("c", normalise, "B", c)
            stage("b", project_k, "B", b, rope_t, [("rope_t_b", b)])
            stage("a", scores, "A", a, mask_add[a % 2], [("mask", a)])
            stage("c", transpose_o, "B", c)
            stage("b", project_q, "B", b, rope_t, [("rope_t_b", b)])
            stage("m", expert_pair, m, 1)
            stage("c", lambda: finish_b(c, *project_o("B", c)))
            stage("a", scores_t, "A", a, mask_add[a % 2])
            stage("b", project_v, "B", b, y_t, [("y_t_b", b)])
            stage("b", spread_queries_b, "B", b)
            stage("m", expert_pair, m, 2)
            stage("b", scores, "B", b, causal_add, [("c_causal", 0)])
            stage("a", attend, "A", a)
            if it + 1 < tiles:
                steps.stream = "A"
                prepare(it + 1)
            stage("b", scores_t, "B", b, causal_add)
            stage("a", normalise, "A", a)
            stage("m", expert_pair, m, 3)
            stage("m", finish, m)
            stage("n", transposed, u[c % 2], u_t, "u_t", c, [("u", c)], [("e_mm3", c - 1)])
            stage("a", transpose_o, "A", a)
            stage("n", gate, c)
            stage("a", lambda: finish_a(a, *project_o("A", a)))
            stage("n", transpose_gates, c)
            stage("n", expert_bias_sum, c)
            if it == 0:
                steps.stream = "setup"
                load_weights_b()
            if it == 1:
                steps.stream = "setup"
                load_experts()
        sp.wait(("store0", tiles - 2 + tiles % 2), ("store1", tiles - 1 - tiles % 2))

        block = ctx.enter_context(nc.Block())
        block.sync(sp.emit)
        block.tensor(pe.emit)
        block.scalar(act.emit)
        block.vector(dve.emit)
        block.gpsimd(pool.emit)


def constants():
    inv_freq = np.float32(1.0) / np.float32(10000.0) ** (
        np.arange(0, HEAD_DIM, 2, dtype=np.float32) / np.float32(HEAD_DIM))
    freqs = np.arange(P, dtype=np.float32)[:, None] * inv_freq[None, :]
    cos = np.tile(np.repeat(np.cos(freqs), 2, axis=1), (1, HEADS)).astype(np.float32)
    sin = np.stack([-np.sin(freqs), np.sin(freqs)], axis=-1).reshape(P, HEAD_DIM)
    sin = np.tile(sin, (1, HEADS)).astype(np.float32)
    head_rows = (np.arange(P)[:, None] // HEAD_DIM == np.arange(HEADS_PER_CHUNK)[None, :]).astype(np.float32)
    return {"rope_cos": cos, "rope_sin": sin, "head_rows": head_rows}


def kernel(**inputs):
    from concourse import bacc
    from concourse.bass_utils import run_bass_kernel_spmd

    a = {k: np.asarray(v) for k, v in inputs.items()}
    x = a["x"]
    mask = a["mask_Bx1xSxS2_bk1"][:, 0]
    arrays = {
        "x": x,
        "ctxT": a["ctx_1024"].transpose(0, 2, 1),
        "masks": np.stack([mask, mask.transpose(0, 2, 1)], axis=1),
        "WqT": a["L0_xattn_Wq"].T, "WkT": a["L0_xattn_Wk"].T, "WvT": a["L0_xattn_Wv"].T, "WoT": a["L0_xattn_Wo"].T,
        "in_projT": a["L0_ffn_in_proj_w"].T, "out_projT": a["L0_ffn_out_proj_w"].T, "gate_wT": a["L0_ffn_gate_w"].T,
        "expertsT": a["L0_ffn_expert_w"].transpose(2, 0, 1).reshape(EMBED, EXPERTS * EMBED),
    }
    for name in ("g_xattn", "g_ffn", "L0_xattn_bq", "L0_xattn_bk", "L0_xattn_bv", "L0_xattn_bo",
                 "L0_ffn_in_proj_b", "L0_ffn_out_proj_b", "L0_ffn_gate_b", "L0_ffn_expert_b",
                 "L0_ffn_ln1_w", "L0_ffn_ln1_b", "L0_ffn_ln2_w", "L0_ffn_ln2_b"):
        arrays[name] = a[name]
    arrays.update(constants())
    arrays = {k: np.ascontiguousarray(v) for k, v in arrays.items()}

    nc = bacc.Bacc("TRN2", target_bir_lowering=False, num_devices=1)
    dram = {k: nc.dram_tensor(f"in_{k}", v.shape, mybir.dt.from_np(v.dtype), kind="ExternalInput").ap()
            for k, v in arrays.items()}
    out = nc.dram_tensor("out", x.shape, F32, kind="ExternalOutput").ap()
    build(nc, dram, out)
    result = run_bass_kernel_spmd(nc, [{f"in_{k}": v for k, v in arrays.items()}], core_ids=[0])
    return result.results[0]["out"]
```

```python
from contextlib import ExitStack
from functools import partial

import numpy as np

import concourse.bass as bass
from concourse import mybir

ALU = mybir.AluOpType
ACT = mybir.ActivationFunctionType
AXIS_X = mybir.AxisListType.X
F32 = mybir.dt.float32
F32R = mybir.dt.float32r
BF16 = mybir.dt.bfloat16

P = 128
EMBED = 256
HEADS = 16
HEAD_DIM = EMBED // HEADS
CHUNKS = EMBED // P
PARTS = 3
HEAD_ROWS = PARTS * HEAD_DIM
PAIRS = HEADS // 2
PAIR_ROWS = 2 * HEAD_ROWS
BANK = 512
GROUP = BANK // P
GROUPS = HEADS // GROUP
STRIP = 32
EXPERTS = 8
SCALE = HEAD_DIM ** -0.5
EPS = 1e-5
MASKED = -(2.0 ** 100)
READER_FIRST = "a bank's last reader must be queued before the bank is taken again"


ROUND = (
    ("A_pairs_k0", 0), ("B_rope", 1), ("A_pairs_k1", 0), ("M_finish", 4), ("B_normalise", 2), ("M_gates_t", 3),
    ("A_pairs_k1", 0), ("M_bias", 3), ("A_spread_k0", 0), ("A_spread_k1", 0), ("M_pair0", 3),
    ("B_normalise", 2), ("A_pairs_q0", 0), ("A_pairs_q0", 0), ("M_bias", 3), ("M_sum0", 3), ("A_pairs_q1", 0),
    ("A_pairs_q1", 0), ("A_ctx", -1), ("B_o_t", 2), ("B_rope_t", 1), ("A_spread_q", 0), ("B_rope_t", 1),
    ("B_y_t", 1), ("B_base", 2), ("B_o_t", 2), ("A_scores", 0), ("B_y_t", 1), ("B_qk", 1), ("A_scores", 0),
    ("M_pair1", 3), ("B_qk", 1), ("A_scores_t", 0), ("A_max", 0), ("B_split_q", 1), ("B_out", 2),
    ("B_split_k", 1), ("A_norm", -1), ("M_sum1", 3), ("B_pairs_q1", 1), ("B_finish", 2), ("B_pairs_q0", 1),
    ("A_xn", -1), ("B_norm_1", 2), ("B_pairs_q1", 1), ("B_pairs_q0", 1), ("B_pairs_k1", 1), ("B_pairs_k0", 1),
    ("A_max_t", 0), ("B_pairs_k1", 1), ("B_pairs_k0", 1), ("B_v", 1), ("B_v", 1), ("B_spread_q", 1),
    ("A_max_t", 0), ("B_spread_k0", 1), ("B_norm_1", 2), ("A_base", 0), ("M_pair2", 3), ("A_exp", 0),
    ("B_spread_k1", 1), ("A_exp", 0), ("B_scores", 1), ("A_mask", -1), ("M_sum2", 3), ("B_scores", 1),
    ("B_max", 1), ("A_attend", 0), ("B_scores_t", 1), ("A_attend", 0), ("B_max_t", 1), ("A_normalise", 0),
    ("B_max_t", 1), ("A_normalise", 0), ("B_exp", 1), ("B_exp", 1), ("M_pair3", 3), ("A_o_t", 0), ("M_u_t", 2),
    ("M_sum3", 3), ("A_o_t", 0), ("M_u_t", 2), ("A_x_t", -1), ("B_causal3", 1), ("B_causal0", 1), ("A_out", 0),
    ("A_x_t", -1), ("B_causal1", 1), ("A_kv", -1), ("B_causal2", 1), ("M_norm_2", 3), ("M_gate", 2),
    ("A_finish", 0), ("B_attend", 1), ("A_kv", -1), ("A_split_k", -1), ("M_gate", 2), ("M_gate_rank", 2),
    ("B_attend", 1), ("A_q", -1), ("A_pairs_k0", -1), ("A_q", -1), ("M_gate_choice", 2), ("M_gates_t", 2),
    ("A_split_q", -1),
)


class Steps:

    def __init__(self, nc, ctx):
        self.nc, self.ctx = nc, ctx
        self.stream = "setup"
        self.sems, self.count, self.done = {}, {}, {}

    def count_up(self, sem, name, tile, by):
        if sem not in self.sems:
            self.sems[sem] = self.ctx.enter_context(self.nc.semaphore("s_" + sem))
            self.count[sem] = 0
        self.count[sem] += by
        self.done[name, tile] = (sem, self.count[sem])
        return self.sems[sem]


class Queue:

    def __init__(self, steps, name):
        self.steps, self.name, self.items, self.seen = steps, name, [], {}

    def wait(self, *keys):
        need = {}
        for name, tile in keys:
            if tile >= 0:
                sem, value = self.steps.done[name, tile]
                need[sem] = max(need.get(sem, 0), value)
        for sem, value in need.items():
            if self.seen.get(sem, 0) < value:
                self.seen[sem] = value
                self.items.append(lambda eng, s=self.steps.sems[sem], v=value: eng.wait_ge(s, v))

    def do(self, call, name=None, tile=0):
        if name is None:
            self.items.append(call)
        else:
            sem = self.steps.count_up(f"{self.name}_{self.steps.stream}", name, tile, 1)
            self.items.append(lambda eng: call(eng).then_inc(sem, 1))

    def dma(self, call, name, tile=0):
        sem = self.steps.count_up(name, name, tile, 16)
        self.items.append(lambda eng: call(eng).then_inc(sem, 16))

    def emit(self, eng):
        for item in self.items:
            item(eng)


def build(nc, dram, out):
    tiles = out.shape[0]
    with ExitStack() as ctx:
        def sb(name, shape, dt=F32):
            return ctx.enter_context(nc.sbuf_tensor(name, shape, dt))

        steps = Steps(nc, ctx)
        sp, pe, act, dve, pool = (Queue(steps, n) for n in ("sp", "pe", "act", "dve", "pool"))

        x_in = [sb(f"x_in{i}", [P, EMBED]) for i in range(3)]
        ctx_t = [sb(f"ctx_t{i}", [P, CHUNKS, P]) for i in range(2)]
        mask_u8 = [sb(f"mask_u8{i}", [P, 2, P], mybir.dt.uint8) for i in range(3)]
        mask_add = [sb(f"mask_add{i}", [P, 2, P], BF16) for i in range(2)]
        causal_add = sb("causal_add", [P, 1, P], BF16)
        ident = sb("ident", [P, P])
        ident_bf = sb("ident_bf", [P, P], BF16)
        pick = sb("pick", [P, HEADS, P], BF16)
        ident_r = sb("ident_r", [P, P], F32R)
        head_rows = sb("head_rows", [P, 2])
        lower_tri = sb("lower_tri", [P, EXPERTS, EXPERTS])
        rope_cos = sb("rope_cos", [P, EMBED])
        rope_sin = sb("rope_sin", [P, EMBED])
        neg_half = sb("neg_half", [P, 1])

        widths = {"Aq": EMBED, "Akv": 2 * EMBED, "Ao": EMBED, "Bqk": 2 * EMBED, "Bv": EMBED, "Bo": EMBED}
        weight = {m: [sb(f"w_{m}{part}", [P, CHUNKS, width], F32R) for part in "ab"] for m, width in widths.items()}
        experts_w = [sb(f"w_experts{part}", [P, CHUNKS, EXPERTS * EMBED], F32R) for part in "ab"]
        gate_f = sb("gate_f", [P, CHUNKS, EXPERTS])
        gate_w = [sb(f"w_gate{part}", [P, CHUNKS, EXPERTS], F32R) for part in "ab"]
        w_stage = [sb(f"w_stage{i}", [P, CHUNKS, EMBED]) for i in range(2)]
        expert_bias = sb("expert_bias", [P, EMBED])
        rows = {n: sb(f"row_{n}", [P, EMBED]) for n in
                ("bq_A", "bk_A", "bv_A", "bo_A", "bv_B", "bo_B", "ln1_w", "ln1_b", "ln2_w", "ln2_b")}
        bqk_B = sb("row_bqk_B", [P, 2 * EMBED])
        gate_bias = sb("gate_bias", [P, EXPERTS])
        gains = sb("gains", [P, 2])
        tanh_gains = sb("tanh_gains", [P, 2])

        stats = {n: sb(f"stats_{n}", [P, 6]) for n in ("A", "B", "1", "2")}
        mean_var = {n: sb(f"mean_var_{n}", [P, 2]) for n in ("A", "B", "1", "2")}
        var_eps = {n: sb(f"var_eps_{n}", [P, 1]) for n in ("A", "B", "1", "2")}
        rstd = {n: sb(f"rstd_{n}", [P, 1]) for n in ("A", "B", "1", "2")}

        xn = sb("xn", [P, EMBED])
        yn = [sb(f"yn{i}", [P, EMBED]) for i in range(3)]
        roped = sb("roped", [P, EMBED])
        rope_tmp = sb("rope_tmp", [P, EMBED])
        u_n = sb("u_n", [P, EMBED])
        u = [sb(f"u{i}", [P, EMBED]) for i in range(2)]
        x1 = [sb(f"x1_{i}", [P, EMBED]) for i in range(5)]
        base = {t: sb(f"base_{t}", [P, EMBED]) for t in "AB"}

        def parts(name, cols_):
            return [sb(f"{name}_{part}", [P, cols_], F32R) for part in "ab"]

        xn_t, ctx_ab, rope_t, y_t, u_t = (parts(n, EMBED) for n in ("xn_t", "ctx_ab", "rope_t", "y_t", "u_t"))
        qk_f = {t: sb(f"qk_f_{t}", [P, 2 * EMBED]) for t in "AB"}
        qk_parts = {w: sb(f"{w}_parts", [P, HEADS, PARTS, HEAD_DIM], F32R) for w in "qk"}
        pairs_of = {t: {w: sb(f"{w}_pairs_{t}", [PAIR_ROWS, PAIRS, P], F32R) for w in "qk"} for t in "AB"}
        q_spread = {t: sb(f"q_spread_{t}", [PAIR_ROWS, PAIRS, 2, P], F32R) for t in "AB"}
        k_spread = sb("k_spread", [PAIR_ROWS, PAIRS, 2, P], F32R)
        values = {t: sb(f"values_{t}", [P, HEADS, STRIP]) for t in "AB"}
        neg_max = {t: sb(f"neg_max_{t}", [P, HEADS]) for t in "AB"}
        neg_max_bf = {t: sb(f"neg_max_bf_{t}", [P, P], BF16) for t in "AB"}
        neg_max_t = {t: sb(f"neg_max_t_{t}", [P, P], BF16) for t in "AB"}
        probs = {t: sb(f"probs_{t}", [P, HEADS, P]) for t in "AB"}
        o_raw = sb("o_raw", [P, BANK])
        inv_sum = {t: sb(f"inv_sum_{t}", [P, HEADS]) for t in "AB"}
        o_norm = {t: sb(f"o_norm_{t}", [P, EMBED]) for t in "AB"}
        o_t = {t: parts(f"o_t_{t}", EMBED) for t in "AB"}

        logits = sb("logits", [P, EXPERTS])
        neg_top = sb("neg_top", [P, 1])
        gate_exp = sb("gate_exp", [P, EXPERTS])
        gate_sum = sb("gate_sum", [P, 1])
        gate_inv = sb("gate_inv", [P, 1])
        beats = sb("beats", [P, EXPERTS, EXPERTS])
        equals = sb("equals", [P, EXPERTS, EXPERTS])
        rank = sb("rank", [P, EXPERTS])
        chosen = sb("chosen", [P, EXPERTS])
        gates = sb("gates", [P, P])
        gates_t = sb("gates_t", [P, P])
        moe = [sb(f"moe{i}", [P, EMBED]) for i in range(2)]
        v_n = sb("v_n", [P, EMBED])
        y_out = sb("y_out", [P, EMBED])

        banks = [ctx.enter_context(nc.psum_tensor(f"bank{i}", [P, BANK], F32)) for i in range(8)]
        score_banks, pv_bank = banks[0:GROUPS], banks[6]
        work_banks = [banks[4], banks[5], banks[7]]
        score_free = [[] for _ in range(GROUPS)]
        pv_free = []
        work_free = [[] for _ in work_banks]
        work_turn = [0]

        def take_work():
            n = work_turn[0] % len(work_banks)
            work_turn[0] += 1
            assert work_free[n] is not None, READER_FIRST
            pe.wait(*work_free[n])
            work_free[n] = None
            return n, work_banks[n]

        def products(out_ap, left, right):
            calls = [(l, r) for (la, lb), (ra, rb) in zip(left, right) for l, r in ((la, ra), (la, rb), (lb, ra))]
            for n, (l, r) in enumerate(calls):
                fn = (lambda eng, l=l, r=r, s=n == 0, e=n == len(calls) - 1:
                      eng.matmul(out_ap, l, r, start=s, stop=e))
                if n < len(calls) - 1:
                    pe.do(fn)
            return fn

        def chunk(pair, c):
            return tuple(x[:, c * P:(c + 1) * P] for x in pair)

        def by_head(ap):
            return ap.rearrange("p (h d) -> p h d", d=HEAD_DIM)

        order = {m: n for n, m in enumerate(["Ak", "Av", "Aq", "Ao", "Bq", "Bk", "Bv", "Bo"] +
                                            [f"E{e}" for e in range(EXPERTS)])}

        def load(dst, src, name, tile=0):
            sp.dma(lambda eng: eng.dma_start(dst, src), name, tile)

        def load_row(dst, src, name):
            load(dst, src.rearrange("(a n) -> a n", a=1).to_broadcast([P, src.shape[0]]), name)

        first_rows = ("bq_A", "bk_A", "bv_A")
        row_src = {"bq_A": dram["L0_xattn_bq"], "bk_A": dram["L0_xattn_bk"], "bv_A": dram["L0_xattn_bv"],
                   "bo_A": dram["L0_xattn_bo"],
                   "bv_B": dram["L0_ffn_in_proj_b"][2 * EMBED:3 * EMBED], "bo_B": dram["L0_ffn_out_proj_b"],
                   "ln1_w": dram["L0_ffn_ln1_w"], "ln1_b": dram["L0_ffn_ln1_b"],
                   "ln2_w": dram["L0_ffn_ln2_w"], "ln2_b": dram["L0_ffn_ln2_b"]}

        def split_weight(n, src, dst):
            slot = n % len(w_stage)
            sp.wait(("w_b", n - len(w_stage)))
            load(w_stage[slot][:], src.rearrange("(c p) n -> p c n", p=P), f"ld_w{slot}", n)
            act.wait((f"ld_w{slot}", n))
            act.do(lambda eng: eng.activation(dst[0], w_stage[slot][:], ACT.Copy), "w_a", n)
            dve.wait(("w_a", n))
            dve.do(lambda eng: eng.tensor_tensor(dst[1], w_stage[slot][:], dst[0].bitcast(F32), ALU.subtract),
                   "w_b", n)

        def setup():
            load(head_rows[:], dram["head_rows"], "ld_head")
            pool.do(lambda eng: eng.memset(ident[:], 0.0), "c_zero")
            pool.do(lambda eng: eng.memset(neg_half[:], -0.5), "c_zero")
            pool.do(lambda eng: eng.memset(expert_bias[:], 0.0), "c_zero_bias")
            pool.wait(("c_zero", 0))
            pool.do(lambda eng: eng.affine_select(out=ident[:], in_=ident[:], compare_op=ALU.not_equal, fill=1.0,
                                                  base=0, pattern=[[-1, P]], channel_multiplier=1), "c_ident")
            for t in "AB":
                dve.do(lambda eng, t=t: eng.memset(values[t][:], 1.0), "c_dve")
                dve.do(lambda eng, t=t: eng.memset(neg_max_bf[t][:], 0.0), "c_dve")
            dve.do(lambda eng: eng.memset(gates[:], 0.0), "c_dve")
            dve.wait(("c_ident", 0), ("c_dve", 0))
            dve.do(lambda eng: eng.tensor_copy(ident_bf[:], ident[:]), "c_ident_bf")
            dve.do(lambda eng: eng.tensor_copy(ident_r[:], ident[:]), "c_ident_bf")
            for r in first_rows:
                load_row(rows[r][:], row_src[r], "ld_rows_A")

        def setup_more():
            pool.do(lambda eng: eng.memset(pick[:], 0.0), "c_zero")
            pool.do(lambda eng: eng.memset(causal_add[:], 0.0), "c_zero")
            pool.do(lambda eng: eng.memset(lower_tri[:], 1.0), "c_zero")
            pool.wait(("c_zero", 0))
            for n in range(2):
                pool.do(lambda eng, n=n: eng.affine_select(out=pick[:], in_=pick[:], compare_op=ALU.not_equal,
                                                           fill=1.0, base=-n * HEADS, pattern=[[-1, HEADS], [0, P]],
                                                           channel_multiplier=1), "c_pick")
                pool.wait(("c_pick", 0))
            pool.do(lambda eng: eng.affine_select(
                out=causal_add[:, 0, :], in_=causal_add[:, 0, :], compare_op=ALU.is_ge, fill=MASKED, base=0,
                pattern=[[-1, P]], channel_multiplier=1), "c_causal")
            pool.do(lambda eng: eng.affine_select(out=lower_tri[:], in_=lower_tri[:], compare_op=ALU.is_gt, fill=0.0,
                                                  base=0, pattern=[[1, EXPERTS], [-1, EXPERTS]],
                                                  channel_multiplier=0), "c_tri")
            sp.wait(("c_zero_bias", 0))
            for r, src in row_src.items():
                if r not in first_rows:
                    load_row(rows[r][:], src, "ld_rows")
            load_row(bqk_B[:], dram["L0_ffn_in_proj_b"][0:2 * EMBED], "ld_rows")
            load_row(gate_bias[:], dram["L0_ffn_gate_b"], "ld_rows")
            load(expert_bias[0:EXPERTS, :], dram["L0_ffn_expert_b"], "ld_eb")
            load(gate_f[:], dram["gate_wT"].rearrange("(c p) n -> p c n", p=P), "ld_rows")
            load(rope_cos[:], dram["rope_cos"], "ld_cos")
            load(rope_sin[:], dram["rope_sin"], "ld_sin")
            for n, g in enumerate(("g_xattn", "g_ffn")):
                load_row(gains[:, n:n + 1], dram[g], f"ld_gain{n}")
            act.wait(("ld_gain0", 0), ("ld_gain1", 0))
            act.do(lambda eng: eng.activation(tanh_gains[:], gains[:], ACT.Tanh), "c_tanh")
            act.wait(("ld_rows", 0))
            act.do(lambda eng: eng.activation(gate_w[0][:], gate_f[:], ACT.Copy), "w_gate_a")
            pool.wait(("w_gate_a", 0))
            pool.do(lambda eng: eng.tensor_tensor(gate_w[1][:], gate_f[:], gate_w[0][:].bitcast(F32), ALU.subtract),
                    "w_gate_b")
            pool.wait(("c_tanh", 0), ("ld_rows", 0))
            for r, g in (("bo_A", 0), ("ln2_w", 1), ("ln2_b", 1)):
                pool.do(lambda eng, r=r, g=g: eng.tensor_scalar(rows[r][:], rows[r][:], tanh_gains[:, g:g + 1], 1.0,
                                                                ALU.mult, ALU.mult), "c_fold")

        weight_src = {"Aq": (dram["WqT"], "Aq", 0), "Ak": (dram["WkT"], "Akv", 0), "Av": (dram["WvT"], "Akv", 1),
                      "Ao": (dram["WoT"], "Ao", 0), "Bq": (dram["in_projT"][:, 0:EMBED], "Bqk", 0),
                      "Bk": (dram["in_projT"][:, EMBED:2 * EMBED], "Bqk", 1),
                      "Bv": (dram["in_projT"][:, 2 * EMBED:3 * EMBED], "Bv", 0), "Bo": (dram["out_projT"], "Bo", 0)}

        def load_weights(names):
            for m in names:
                if m[0] == "E":
                    cut = slice(int(m[1:]) * EMBED, (int(m[1:]) + 1) * EMBED)
                    split_weight(order[m], dram["expertsT"][:, cut], [w[:, :, cut] for w in experts_w])
                else:
                    src, mat, half = weight_src[m]
                    split_weight(order[m], src, [w[:, :, half * EMBED:(half + 1) * EMBED] for w in weight[mat]])

        def load_tile(t):
            s = t % 3
            sp.wait(("A_base", t - 3), ("xn", t - 3), ("ctx_b", t - 2), ("mask", t - 3))
            sp.dma(lambda eng: eng.dma_start(x_in[s][:], dram["x"][t]), f"ld_x{s}", t)
            sp.dma(lambda eng: eng.dma_start(ctx_t[t % 2][:], dram["ctxT"][t].rearrange("(c p) k -> p c k", p=P)),
                  f"ld_c{t % 2}", t)
            sp.dma(lambda eng: eng.dma_start(mask_u8[s][:], dram["masks"][t].rearrange("m p k -> p m k")),
                  f"ld_m{s}", t)

        def norm_stats(n, t, src, ready, name):
            dve.wait(*ready)
            dve.do(lambda eng: eng.bn_stats(stats[n][:], src[:]), f"st_{n}", t)
            dve.wait((f"st_{n}", t), (f"ve_{n}", t - 1), (name, t - 1))
            dve.do(lambda eng: eng.bn_aggr(mean_var[n][:], stats[n][:]), f"mv_{n}", t)
            pool.wait((f"mv_{n}", t))
            pool.do(lambda eng: eng.tensor_scalar(var_eps[n][:], mean_var[n][:, 1:2], EPS, 1.0, ALU.add, ALU.mult),
                    f"ve_{n}", t)
            pool.wait((f"ve_{n}", t), (name, t - 1))
            pool.do(lambda eng: eng.tensor_tensor(rstd[n][:], var_eps[n][:], neg_half[:], ALU.pow), f"rstd_{n}", t)

        def norm_apply(n, t, src, dst, free, name):
            dve.wait((f"rstd_{n}", t), *free)
            dve.do(lambda eng: eng.tensor_scalar(dst[:], src[:], mean_var[n][:, 0:1], rstd[n][:], ALU.subtract,
                                                 ALU.mult), name, t)

        def split_out(n_bank, src, dst, name, t, ready, free):
            act.wait(ready, *free)
            act.do(lambda eng: eng.activation(dst[0], src, ACT.Copy), name + "_a", t)
            dve.wait((name + "_a", t))
            dve.do(lambda eng: eng.tensor_tensor(dst[1], src, dst[0].bitcast(F32), ALU.subtract), name + "_b", t)
            work_free[n_bank] = [(name + "_b", t)]

        def transposed(src, dst, name, t, ready, free):
            n, bank = take_work()
            pe.wait(*ready, ("c_ident", 0))
            for c in range(CHUNKS):
                pe.do(lambda eng, c=c: eng.transpose(bank[:, c * P:(c + 1) * P], src[:, c * P:(c + 1) * P], ident[:]),
                      *((name + "_tp", t) if c == CHUNKS - 1 else ()))
            yield
            split_out(n, bank[:, 0:EMBED], [d[:] for d in dst], name, t, (name + "_tp", t), free)

        def prepare_norm(t):
            norm_stats("A", t, x_in[t % 3], [(f"ld_x{t % 3}", t)], "xn")

        def prepare_ctx(t):
            pool.wait((f"ld_c{t % 2}", t), ("Akv_mm", t - 1))
            ctx_flat = ctx_t[t % 2][:].rearrange("p c k -> p (c k)")
            pool.do(lambda eng: eng.tensor_copy(ctx_ab[0][:], ctx_flat), "ctx_a", t)
            pool.wait(("ctx_a", t))
            pool.do(lambda eng: eng.tensor_tensor(ctx_ab[1][:], ctx_flat, ctx_ab[0][:].bitcast(F32), ALU.subtract),
                    "ctx_b", t)

        def prepare_mask(t):
            pool.wait((f"ld_m{t % 3}", t), ("A_st", t - 2))
            pool.do(lambda eng: eng.tensor_scalar(mask_add[t % 2][:], mask_u8[t % 3][:], MASKED, 1.0, ALU.mult,
                                                  ALU.mult), "mask", t)

        def prepare_x(t):
            norm_apply("A", t, x_in[t % 3], xn, [("xn_tp", t - 1)], "xn")

        def project(mat, t, src, ready, last_weight):
            n, bank = take_work()
            pe.wait(*ready, ("w_b", order[last_weight]))
            last = products(bank[:, 0:widths[mat]], [chunk(src, c) for c in range(CHUNKS)],
                            [tuple(w[:, c, :] for w in weight[mat]) for c in range(CHUNKS)])
            pe.do(last, mat + "_mm", t)
            return n, bank

        def add_bias(tag, mat, step, cut, t, src, bias, bias_ready):
            dve.wait((mat + "_mm", t), bias_ready, *[(f"{tag}{w}_b", t - 1) for w in "qk"])
            dve.do(lambda eng: eng.tensor_tensor(qk_f[tag][:, cut], src, bias, ALU.add), step, t)

        def add_values(tag, mat, t, src, bias_ready):
            dve.wait((mat + "_mm", t), (tag + "_pv", t - 1), bias_ready, ("c_dve", 0))
            dve.do(lambda eng: eng.tensor_tensor(values[tag][:, :, 0:HEAD_DIM], by_head(src),
                                                 by_head(rows["bv_" + tag][:]), ALU.add), tag + "_v", t)

        def project_q_a(t):
            n, bank = project("Aq", t, xn_t, [("xn_b", t)], "Aq")
            yield
            add_bias("A", "Aq", "Aq_f", slice(0, EMBED), t, bank[:, 0:EMBED], rows["bq_A"][:], ("ld_rows_A", 0))
            work_free[n] = [("Aq_f", t)]

        def project_kv_a(t):
            n, bank = project("Akv", t, ctx_ab, [("ctx_b", t)], "Av")
            yield
            add_bias("A", "Akv", "Ak_f", slice(EMBED, 2 * EMBED), t, bank[:, 0:EMBED], rows["bk_A"][:],
                     ("ld_rows_A", 0))
            add_values("A", "Akv", t, bank[:, EMBED:2 * EMBED], ("ld_rows_A", 0))
            work_free[n] = [("A_v", t)]

        def project_qk_b(t):
            n, bank = project("Bqk", t, rope_t, [("rope_t_b", t)], "Bk")
            yield
            add_bias("B", "Bqk", "Bqk_f", slice(0, 2 * EMBED), t, bank[:], bqk_B[:], ("ld_rows", 0))
            work_free[n] = [("Bqk_f", t)]

        def project_v_b(t):
            n, bank = project("Bv", t, y_t, [("y_t_b", t)], "Bv")
            yield
            add_values("B", "Bv", t, bank[:, 0:EMBED], ("ld_rows", 0))
            work_free[n] = [("B_v", t)]

        def before(tag, t):
            return ("B", t - 2) if tag == "A" else ("A", min(t + 1, tiles - 1))

        def split_heads(tag, w, t):
            half = by_head(qk_f[tag][:, EMBED * "qk".index(w):EMBED * ("qk".index(w) + 1)])
            other, tile = before(tag, t)
            act.wait(("Bqk_f" if tag == "B" else f"A{w}_f", t), (f"{other}{w}_tp1", tile))
            again, rest = (2, 1) if w == "q" else (1, 2)
            for part in (0, again):
                act.do(lambda eng, part=part: eng.activation(qk_parts[w][:, :, part, :], half, ACT.Copy),
                       f"{tag}{w}_a", t)
            pool.wait((f"{tag}{w}_a", t))
            pool.do(lambda eng: eng.tensor_tensor(qk_parts[w][:, :, rest, :], half,
                                                  qk_parts[w][:, :, 0, :].bitcast(F32), ALU.subtract),
                    f"{tag}{w}_b", t)

        spread_steps = {"q": lambda tag: [tag + "q_spread"], "k": lambda tag: [f"{tag}k_spread{j}" for j in range(2)]}

        def transpose_heads(tag, w, g, t):
            flat = qk_parts[w][:].rearrange("p h s d -> p (h s d)")
            n, bank = take_work()
            pe.wait((f"{tag}{w}_b", t), ("c_ident_bf", 0))
            for i in range(PAIRS // 2):
                pair = g * PAIRS // 2 + i
                pe.do(lambda eng, i=i, pair=pair: eng.transpose(
                    bank[0:PAIR_ROWS, i * P:(i + 1) * P].bitcast(F32R),
                    flat[:, pair * PAIR_ROWS:(pair + 1) * PAIR_ROWS], ident_r[:]),
                    *((f"{tag}{w}_tp{g}", t) if i == PAIRS // 2 - 1 else ()))
            half = slice(g * PAIRS // 2, (g + 1) * PAIRS // 2)
            src = bank[0:PAIR_ROWS, :].rearrange("r (i n) -> r i n", n=P)
            yield
            act.wait((f"{tag}{w}_tp{g}", t), *[(step, t - 1) for step in spread_steps[w](tag)],
                     (f"{tag}_s{GROUPS - 1}", t - 1) if w == "q" else (tag + "_st", t - 1))
            act.do(lambda eng: eng.activation(pairs_of[tag][w][:, half, :], src, ACT.Copy), f"{tag}{w}_pairs{g}", t)
            work_free[n] = [(f"{tag}{w}_pairs{g}", t)]

        def spread_queries(tag, t):
            dve.wait((tag + "q_pairs0", t), (tag + "q_pairs1", t), (tag + "_st", t - 1), ("ld_head", 0))
            for j in range(2):
                dve.do(lambda eng, j=j: eng.tensor_scalar(
                    q_spread[tag][:, :, j, :], pairs_of[tag]["q"][:].bitcast(F32),
                    head_rows[0:PAIR_ROWS, j:j + 1], None, ALU.mult), tag + "q_spread", t)

        def spread_keys(tag, j, t):
            other, tile = before(tag, t)
            act.wait((tag + "k_pairs0", t), (tag + "k_pairs1", t), (f"{other}_s{GROUPS - 1}", tile), ("ld_head", 0))
            act.do(lambda eng: eng.activation(k_spread[:, :, j, :], pairs_of[tag]["k"][:].bitcast(F32), ACT.Copy,
                                              scale=head_rows[0:PAIR_ROWS, j:j + 1]), f"{tag}k_spread{j}", t)

        def add_mask(g, add):
            pe.do(lambda eng: eng.matmul(score_banks[g][:], ident_bf[:], add.unsqueeze(1).to_broadcast([P, GROUP, P]),
                                         start=True, stop=False, skip_group_check=True))

        def take_scores(g):
            assert score_free[g] is not None, READER_FIRST
            pe.wait(*score_free[g])
            score_free[g] = None

        def pair_scores(g, left, right, first, last, *done):
            for i in range(2):
                pair = 2 * g + i
                pe.do(lambda eng, i=i, pair=pair: eng.matmul(
                    score_banks[g][:, i * 2 * P:(i + 1) * 2 * P], left[:, pair, :], right[:, pair, :, :],
                    start=first and i == 0, stop=last, skip_group_check=True), *(done if i == 1 else ()))

        def mask_of(tag, t):
            return (mask_add[t % 2], ("mask", t)) if tag == "A" else (causal_add, ("c_causal", 0))

        def scores(tag, t):
            mask, mask_ready = mask_of(tag, t)
            pe.wait((tag + "q_pairs0", t), (tag + "q_pairs1", t), (tag + "k_spread0", t), (tag + "k_spread1", t),
                    mask_ready, ("c_ident_bf", 0))
            for g in range(GROUPS):
                take_scores(g)
                add_mask(g, mask[:, 0, :])
                pair_scores(g, pairs_of[tag]["q"], k_spread, False, True, f"{tag}_s{g}", t)
            yield
            for g in range(GROUPS):
                dve.wait((f"{tag}_s{g}", t), (tag + "_nm", t - 1))
                dve.do(lambda eng, g=g: eng.tensor_reduce(
                    neg_max[tag][:, g * GROUP:(g + 1) * GROUP],
                    score_banks[g][:].rearrange("p (h k) -> p h k", k=P), AXIS_X, ALU.max, negate=True),
                    f"{tag}_max{g}", t)
                score_free[g] = [(f"{tag}_max{g}", t)]

        def max_parts(tag, t):
            hi, lo = neg_max_bf[tag][:, 0:HEADS], neg_max_bf[tag][:, HEADS:2 * HEADS]
            dve.wait(*[(f"{tag}_max{g}", t) for g in range(GROUPS)], (tag + "_mt_tp", t - 1), ("c_dve", 0))
            dve.do(lambda eng: eng.tensor_copy(hi, neg_max[tag][:]), tag + "_nmh", t)
            dve.wait((tag + "_nmh", t))
            dve.do(lambda eng: eng.tensor_tensor(lo, neg_max[tag][:], hi, ALU.subtract), tag + "_nm", t)

        def scores_t(tag, t):
            pe.wait((tag + "k_pairs0", t), (tag + "k_pairs1", t), (tag + "q_spread", t))
            for g in range(GROUPS):
                take_scores(g)
                if tag == "A":
                    add_mask(g, mask_add[t % 2][:, 1, :])
                pair_scores(g, pairs_of[tag]["k"], q_spread[tag], tag == "B", False,
                            *((tag + "_st", t) if g == GROUPS - 1 else ()))

        def transpose_max(tag, t):
            n, bank = take_work()
            pe.wait((tag + "_nm", t), ("c_ident_bf", 0), ("c_pick", 0))
            pe.do(lambda eng: eng.transpose(bank[:, 0:P // 2].bitcast(BF16), neg_max_bf[tag][:], ident_bf[:]),
                  tag + "_mt_tp", t)
            yield
            act.wait((tag + "_mt_tp", t), (f"{tag}_sm{GROUPS - 1}", t - 1))
            act.do(lambda eng: eng.activation(neg_max_t[tag][:], bank[:, 0:P // 2].bitcast(BF16), ACT.Copy),
                   tag + "_mt", t)
            work_free[n] = [(tag + "_mt", t)]

        def exponentials(tag, t):
            pe.wait((tag + "_mt", t))
            for g in range(GROUPS):
                for j in range(GROUP):
                    h = g * GROUP + j
                    pe.do(lambda eng, g=g, j=j, h=h: eng.matmul(
                        score_banks[g][:, j * P:(j + 1) * P], pick[:, h, :], neg_max_t[tag][:], start=False,
                        stop=True, skip_group_check=True), *((f"{tag}_sm{g}", t) if j == GROUP - 1 else ()))
            yield
            for g in range(GROUPS):
                act.wait((f"{tag}_sm{g}", t), (tag + "_pv", t - 1))
                act.do(lambda eng, g=g: eng.activation(
                    probs[tag][:, g * GROUP:(g + 1) * GROUP, :].rearrange("p h q -> p (h q)"), score_banks[g][:],
                    ACT.Exp, scale=SCALE), f"{tag}_exp{g}", t)
                score_free[g] = [(f"{tag}_exp{g}", t)]

        def causal(g, t):
            part = probs["B"][:, g * GROUP:(g + 1) * GROUP, :]
            pool.wait((f"B_exp{g}", t))
            pool.do(lambda eng: eng.affine_select(out=part, in_=part, compare_op=ALU.is_ge, fill=0.0, base=0,
                                                  pattern=[[0, GROUP], [1, P]], channel_multiplier=-1),
                    f"B_probs{g}", t)

        def attend(tag, t):
            probs_step = {"A": "exp", "B": "probs"}[tag]
            assert None not in pv_free, READER_FIRST
            pe.wait((tag + "_v", t), *pv_free)
            for g in range(GROUPS):
                pe.wait((f"{tag}_{probs_step}{g}", t))
                for j in range(GROUP):
                    h = g * GROUP + j
                    pe.do(lambda eng, g=g, j=j, h=h: eng.matmul(
                        pv_bank[STRIP * j:STRIP * (j + 1), g * P:(g + 1) * P], values[tag][:, h, :],
                        probs[tag][:, h, :], start=True, stop=True, tile_position=(0, STRIP * j)),
                        *((tag + "_pv", t) if h == HEADS - 1 else ()))
            pv_free[:] = [None]
            yield
            other, tile = before(tag, t)
            act.wait((tag + "_pv", t), (other + "_or_tp", tile))
            act.do(lambda eng: eng.activation(o_raw[:], pv_bank[:], ACT.Copy), tag + "_or", t)
            pv_free[:] = [(tag + "_or", t)]

        def normalise(tag, t):
            n, bank = take_work()
            pe.wait((tag + "_or", t))
            for g in range(GROUPS):
                pe.do(lambda eng, g=g: eng.transpose(bank[:, g * P:(g + 1) * P], o_raw[:, g * P:(g + 1) * P],
                                                     ident[:]), *((tag + "_or_tp", t) if g == GROUPS - 1 else ()))
            heads = bank[:].rearrange("p (h s) -> p h s", s=STRIP)
            yield
            dve.wait((tag + "_or_tp", t), (tag + "_on", t - 1))
            dve.do(lambda eng: eng.reciprocal(inv_sum[tag][:].unsqueeze(2), heads[:, :, HEAD_DIM:HEAD_DIM + 1]),
                   tag + "_inv", t)
            dve.wait((tag + "_inv", t), (tag + "_ot_tp", t - 1))
            dve.do(lambda eng: eng.tensor_tensor(by_head(o_norm[tag][:]), heads[:, :, 0:HEAD_DIM],
                                                 inv_sum[tag][:].unsqueeze(2).to_broadcast([P, HEADS, HEAD_DIM]),
                                                 ALU.mult), tag + "_on", t)
            work_free[n] = [(tag + "_on", t)]

        def transpose_o(tag, t):
            return transposed(o_norm[tag], o_t[tag], tag + "_ot", t, [(tag + "_on", t)], [(tag + "o_mm", t - 1)])

        out_bank = {}

        def project_o(tag, t):
            n, bank = take_work()
            pe.wait((tag + "_ot_b", t), ("w_b", order[tag + "o"]))
            pe.do(products(bank[:, 0:EMBED], [chunk(o_t[tag], c) for c in range(CHUNKS)],
                           [tuple(w[:, c, :] for w in weight[tag + "o"]) for c in range(CHUNKS)]), tag + "o_mm", t)
            out_bank[tag] = (n, bank)

        def finish_a(t):
            n, bank = out_bank["A"]
            dve.wait(("Ao_mm", t), ("A_base", t), ("c_tanh", 0), ("out", t - 5))
            dve.do(lambda eng: eng.scalar_tensor_tensor(out=x1[t % 5][:], in0=bank[:, 0:EMBED],
                                                        scalar=tanh_gains[:, 0:1], in1=base["A"][:], op0=ALU.mult,
                                                        op1=ALU.add), "A_res", t)
            work_free[n] = [("A_res", t)]
            norm_stats("B", t, x1[t % 5], [("A_res", t)], "yn")

        def rope(t):
            y = yn[t % 3]
            norm_apply("B", t, x1[t % 5], y, [("B_base", t - 3), ("y_t_tp", t - 3), ("rope2", t - 3)], "yn")
            pairs = y[:].rearrange("p (n two) -> p n two", two=2)
            tmp = rope_tmp[:].rearrange("p (n two) -> p n two", two=2)
            sin = rope_sin[:].rearrange("p (n two) -> p n two", two=2)
            pool.wait(("yn", t), ("rope_t_tp", t - 1), ("ld_cos", 0), ("ld_sin", 0))
            pool.do(lambda eng: eng.tensor_tensor(roped[:], y[:], rope_cos[:], ALU.mult), "rope1", t)
            pool.wait(("rope3", t - 1))
            for n_ in range(2):
                pool.do(lambda eng, n_=n_: eng.tensor_tensor(tmp[:, :, n_:n_ + 1], pairs[:, :, 1 - n_:2 - n_],
                                                             sin[:, :, n_:n_ + 1], ALU.mult), "rope2", t)
            pool.wait(("rope1", t), ("rope2", t))
            pool.do(lambda eng: eng.tensor_tensor(roped[:], roped[:], rope_tmp[:], ALU.add), "rope3", t)

        def base_a(t):
            s = t % 3
            pool.wait((f"ld_x{s}", t), ("c_fold", 0), ("A_res", t - 1))
            pool.do(lambda eng: eng.tensor_tensor(base["A"][:], x_in[s][:], rows["bo_A"][:], ALU.add), "A_base", t)

        def base_b(t):
            pool.wait(("yn", t), ("B_res", t - 1), ("ld_rows", 0))
            pool.do(lambda eng: eng.tensor_tensor(base["B"][:], yn[t % 3][:], rows["bo_B"][:], ALU.add), "B_base", t)

        def finish_b(t):
            n, bank = out_bank["B"]
            dve.wait(("Bo_mm", t), ("B_base", t), ("u", t - 1))
            dve.do(lambda eng: eng.tensor_tensor(u_n[:], bank[:, 0:EMBED], base["B"][:], ALU.add), "B_res", t)
            work_free[n] = [("B_res", t)]
            norm_stats("1", t, u_n, [("B_res", t)], "un")

        def norm_1(t):
            norm_apply("1", t, u_n, u_n, [], "un")
            yield
            pool.wait(("un", t), ("ld_rows", 0))
            pool.do(lambda eng: eng.tensor_tensor(u_n[:], u_n[:], rows["ln1_w"][:], ALU.mult), "ug", t)
            pool.wait(("ug", t), ("moe0", t - 2), ("u_t_tp", t - 2))
            pool.do(lambda eng: eng.tensor_tensor(u[t % 2][:], u_n[:], rows["ln1_b"][:], ALU.add), "u", t)

        def gate(t):
            n, bank = take_work()
            pe.wait(("u_t_b", t), ("w_gate_b", 0))
            pe.do(products(bank[:, 0:EXPERTS], [chunk(u_t, c) for c in range(CHUNKS)],
                           [tuple(w[:, c, :] for w in gate_w) for c in range(CHUNKS)]), "gate_mm", t)
            yield
            dve.wait(("gate_mm", t), ("ld_rows", 0), ("gate_exp", t - 1), ("chosen", t - 1))
            dve.do(lambda eng: eng.tensor_tensor(logits[:], bank[:, 0:EXPERTS], gate_bias[:], ALU.add), "logits", t)
            work_free[n] = [("logits", t)]
            dve.wait(("logits", t))
            dve.do(lambda eng: eng.tensor_reduce(neg_top[:], logits[:], AXIS_X, ALU.max, negate=True), "neg_top", t)

        def gate_rank(t):
            act.wait(("neg_top", t), ("gates", t - 1))
            act.do(lambda eng: eng.activation(gate_exp[:], logits[:], ACT.Exp, bias=neg_top[:], accum_out=gate_sum[:]),
                   "gate_exp", t)
            other = logits[:].unsqueeze(1).to_broadcast([P, EXPERTS, EXPERTS])
            this = logits[:].unsqueeze(2).to_broadcast([P, EXPERTS, EXPERTS])
            dve.do(lambda eng: eng.tensor_tensor(beats[:], other, this, ALU.is_gt), "beats", t)
            dve.do(lambda eng: eng.tensor_tensor(equals[:], other, this, ALU.is_equal), "equals", t)
            dve.wait(("equals", t), ("c_tri", 0))
            dve.do(lambda eng: eng.tensor_tensor(equals[:], equals[:], lower_tri[:], ALU.mult), "equals_low", t)
            dve.wait(("equals_low", t), ("beats", t))
            dve.do(lambda eng: eng.tensor_tensor(beats[:], beats[:], equals[:], ALU.add), "beats_all", t)
            dve.wait(("beats_all", t))
            dve.do(lambda eng: eng.tensor_reduce(rank[:], beats[:], AXIS_X, ALU.add), "rank", t)

        def gate_choice(t):
            dve.wait(("gate_exp", t))
            dve.do(lambda eng: eng.reciprocal(gate_inv[:], gate_sum[:]), "gate_inv", t)
            dve.wait(("rank", t))
            dve.do(lambda eng: eng.scalar_tensor_tensor(out=chosen[:], in0=rank[:], scalar=1.5, in1=gate_exp[:],
                                                        op0=ALU.is_lt, op1=ALU.mult), "chosen", t)
            dve.wait(("chosen", t), ("gate_inv", t), ("gates_tp", t - 1), ("moe8", t - 1), ("c_dve", 0))
            dve.do(lambda eng: eng.tensor_scalar(gates[:, 0:EXPERTS], chosen[:], gate_inv[:], None, ALU.mult),
                   "gates", t)

        def transpose_gates(t):
            n, bank = take_work()
            pe.wait(("gates", t))
            pe.do(lambda eng, bank=bank: eng.transpose(bank[:, 0:P], gates[:], ident[:]), "gates_tp", t)
            yield
            act.wait(("gates_tp", t), ("bias_mm", t - 1))
            act.do(lambda eng, bank=bank: eng.activation(gates_t[:], bank[:, 0:P], ACT.Copy), "gates_t", t)
            work_free[n] = [("gates_t", t)]

        def expert_bias_sum(t):
            n, bank = take_work()
            pe.wait(("gates_t", t), ("ld_eb", 0))
            pe.do(lambda eng: eng.matmul(bank[:, 0:EMBED], gates_t[:], expert_bias[:], start=True, stop=True),
                  "bias_mm", t)
            yield
            dve.wait(("bias_mm", t), ("u", t), ("vn", t - 1))
            dve.do(lambda eng: eng.tensor_tensor(moe[0][:], bank[:, 0:EMBED], u[t % 2][:], ALU.add), "moe0", t)
            work_free[n] = [("moe0", t)]

        pair_bank = {}

        def expert_pair(pair, t):
            n, bank = pair_bank[pair] = take_work()
            cut = slice(pair * 2 * EMBED, (pair + 1) * 2 * EMBED)
            pe.wait(("u_t_b", t), ("w_b", order[f"E{2 * pair + 1}"]))
            pe.do(products(bank[:], [chunk(u_t, c) for c in range(CHUNKS)],
                           [tuple(w[:, c, cut] for w in experts_w) for c in range(CHUNKS)]), f"e_mm{pair}", t)

        def expert_sum(pair, t):
            n, bank = pair_bank[pair]
            dve.wait((f"e_mm{pair}", t))
            for e in (2 * pair, 2 * pair + 1):
                dve.wait((f"moe{e}", t))
                dve.do(lambda eng, e=e: eng.scalar_tensor_tensor(
                    out=moe[(e + 1) % 2][:], in0=bank[:, (e % 2) * EMBED:(e % 2 + 1) * EMBED],
                    scalar=gates[:, e:e + 1], in1=moe[e % 2][:], op0=ALU.mult, op1=ALU.add), f"moe{e + 1}", t)
            work_free[n] = [(f"moe{2 * pair + 2}", t)]

        def finish(t):
            kept = x1[t % 5]
            norm_apply("2", t, moe[0], v_n, [("out", t - 1)], "vn")
            pool.wait(("yn", t), ("c_fold", 0))
            pool.do(lambda eng: eng.tensor_tensor(kept[:], kept[:], rows["ln2_b"][:], ALU.add), "x1_b", t)
            pool.wait(("vn", t))
            pool.do(lambda eng: eng.tensor_tensor(v_n[:], v_n[:], rows["ln2_w"][:], ALU.mult), "vg", t)
            pool.wait(("vg", t), ("x1_b", t), ("store", t - 1))
            pool.do(lambda eng: eng.tensor_tensor(y_out[:], v_n[:], kept[:], ALU.add), "out", t)
            sp.wait(("out", t))
            sp.dma(lambda eng: eng.dma_start(out[t], y_out[:]), "store", t)

        stages = {
            "A_x_t": lambda t: transposed(xn, xn_t, "xn", t, [("xn", t)], [("Aq_mm", t - 1)]),
            "A_kv": project_kv_a, "A_q": project_q_a, "A_base": base_a, "A_finish": finish_a,
            "A_norm": prepare_norm, "A_ctx": prepare_ctx, "A_mask": prepare_mask, "A_xn": prepare_x,
            "B_rope": rope, "B_base": base_b, "B_qk": project_qk_b, "B_v": project_v_b, "B_finish": finish_b,
            "B_norm_1": norm_1,
            "B_rope_t": lambda t: transposed(roped, rope_t, "rope_t", t, [("rope3", t)], [("Bqk_mm", t - 1)]),
            "B_y_t": lambda t: transposed(yn[t % 3], y_t, "y_t", t, [("yn", t)], [("Bv_mm", t - 1)]),
            "M_u_t": lambda t: transposed(u[t % 2], u_t, "u_t", t, [("u", t)], [("e_mm3", t - 1)]),
            "M_gate": gate, "M_gate_rank": gate_rank, "M_gate_choice": gate_choice, "M_gates_t": transpose_gates,
            "M_bias": expert_bias_sum, "M_norm_2": lambda t: norm_stats("2", t, moe[0], [("moe8", t)], "vn"),
            "M_finish": finish}
        for tag in "AB":
            for j in range(2):
                stages[f"{tag}_spread_k{j}"] = partial(spread_keys, tag, j)
            for w in "qk":
                stages[f"{tag}_split_{w}"] = partial(split_heads, tag, w)
                for g in range(2):
                    stages[f"{tag}_pairs_{w}{g}"] = partial(transpose_heads, tag, w, g)
            for name, call in (("spread_q", spread_queries), ("scores", scores), ("max", max_parts),
                               ("scores_t", scores_t), ("max_t", transpose_max), ("exp", exponentials),
                               ("attend", attend), ("normalise", normalise), ("o_t", transpose_o),
                               ("out", project_o)):
                stages[f"{tag}_{name}"] = partial(call, tag)
        for g in range(GROUPS):
            stages[f"B_causal{g}"] = partial(causal, g)
        for pair in range(EXPERTS // 2):
            stages[f"M_pair{pair}"] = partial(expert_pair, pair)
            stages[f"M_sum{pair}"] = partial(expert_sum, pair)

        handed_over = {}

        def run_stage(name, t):
            if 0 <= t < tiles:
                steps.stream = name[0]
                going = handed_over.pop((name, t), None)
                if going is None:
                    going = stages[name](t)
                    if going is not None:
                        next(going)
                        handed_over[name, t] = going
                else:
                    for _ in going:
                        raise AssertionError("a stage yields once")
                steps.stream = "setup"

        load_tile(0)
        setup()
        load_weights(("Ak", "Av", "Aq"))
        for name, lag in ROUND:
            if lag < 0:
                run_stage(name, 0)
        load_tile(1)
        load_weights(("Ao",))
        setup_more()
        to_load = {0: ["Bq", "Bk", "Bv"], 1: ["Bo"] + [f"E{e}" for e in range(4)], 2: [f"E{e}" for e in range(4, 8)]}
        for it in range(tiles + max(lag for _, lag in ROUND)):
            if it + 2 < tiles:
                load_tile(it + 2)
            later = to_load.get(it, [])
            every = len(ROUND) // (len(later) + 1)
            for n, (name, lag) in enumerate(ROUND):
                if later and n % every == every - 1:
                    load_weights([later.pop(0)])
                if lag >= 0 or it - lag > 0:
                    run_stage(name, it - lag)
        sp.wait(("store", tiles - 1))

        block = ctx.enter_context(nc.Block())
        block.sync(sp.emit)
        block.tensor(pe.emit)
        block.scalar(act.emit)
        block.vector(dve.emit)
        block.gpsimd(pool.emit)


def constants():
    inv_freq = np.float32(1.0) / np.float32(10000.0) ** (
        np.arange(0, HEAD_DIM, 2, dtype=np.float32) / np.float32(HEAD_DIM))
    freqs = np.arange(P, dtype=np.float32)[:, None] * inv_freq[None, :]
    cos = np.tile(np.repeat(np.cos(freqs), 2, axis=1), (1, HEADS)).astype(np.float32)
    sin = np.stack([-np.sin(freqs), np.sin(freqs)], axis=-1).reshape(P, HEAD_DIM)
    sin = np.tile(sin, (1, HEADS)).astype(np.float32)
    head_rows = (np.arange(P)[:, None] // HEAD_ROWS == np.arange(2)[None, :]).astype(np.float32)
    return {"rope_cos": cos, "rope_sin": sin, "head_rows": head_rows}


def kernel(**inputs):
    from concourse import bacc
    from concourse.bass_utils import run_bass_kernel_spmd

    a = {k: np.asarray(v) for k, v in inputs.items()}
    x = a["x"]
    mask = a["mask_Bx1xSxS2_bk1"][:, 0]
    arrays = {
        "x": x,
        "ctxT": a["ctx_1024"].transpose(0, 2, 1),
        "masks": np.stack([mask, mask.transpose(0, 2, 1)], axis=1),
        "WqT": a["L0_xattn_Wq"].T, "WkT": a["L0_xattn_Wk"].T, "WvT": a["L0_xattn_Wv"].T, "WoT": a["L0_xattn_Wo"].T,
        "in_projT": a["L0_ffn_in_proj_w"].T, "out_projT": a["L0_ffn_out_proj_w"].T, "gate_wT": a["L0_ffn_gate_w"].T,
        "expertsT": a["L0_ffn_expert_w"].transpose(2, 0, 1).reshape(EMBED, EXPERTS * EMBED),
    }
    for name in ("g_xattn", "g_ffn", "L0_xattn_bq", "L0_xattn_bk", "L0_xattn_bv", "L0_xattn_bo",
                 "L0_ffn_in_proj_b", "L0_ffn_out_proj_b", "L0_ffn_gate_b", "L0_ffn_expert_b",
                 "L0_ffn_ln1_w", "L0_ffn_ln1_b", "L0_ffn_ln2_w", "L0_ffn_ln2_b"):
        arrays[name] = a[name]
    arrays.update(constants())
    arrays = {k: np.ascontiguousarray(v) for k, v in arrays.items()}

    nc = bacc.Bacc("TRN2", target_bir_lowering=False, num_devices=1)
    dram = {k: nc.dram_tensor(f"in_{k}", v.shape, mybir.dt.from_np(v.dtype), kind="ExternalInput").ap()
            for k, v in arrays.items()}
    out = nc.dram_tensor("out", x.shape, F32, kind="ExternalOutput").ap()
    build(nc, dram, out)
    result = run_bass_kernel_spmd(nc, [{f"in_{k}": v for k, v in arrays.items()}], core_ids=[0])
    return result.results[0]["out"]
```
